# Optimizing a Trainium2 kernel written in Bass

```python
import numpy as np
import jax
import jax.numpy as jnp

def _softmax(x, axis=-1):
    return jax.nn.softmax(x, axis=axis)

def _gelu(x):
    return jax.nn.gelu(x, approximate=True)

def _silu(x):
    return jax.nn.silu(x)

def _sigmoid(x):
    return jax.nn.sigmoid(x)

def _layernorm(x, axis=-1, eps=1e-05):
    m = jnp.mean(x, axis=axis, keepdims=True)
    v = jnp.var(x, axis=axis, keepdims=True)
    return (x - m) / jnp.sqrt(v + eps)

def _scatter_add(tgt, idx, src, axis=0):
    return tgt.at[idx].add(src)

def _segment_sum(src, seg, n):
    return jax.ops.segment_sum(src, seg, n)
kernel_name = 'mk_gnn_preln_d2_gnn_r32_e87aa8'

def setup_inputs(seed: int=0):
    np.random.seed(seed)
    _w = jnp.asarray

    def _rec_inputs():
        import jax
        import jax.numpy as jnp
        _gk = jax.random.key(seed)
        x = -0.0001006 + 1 * jax.random.normal(jax.random.fold_in(_gk, 1), (3125, 96), jnp.float32)
        _s = jax.random.randint(jax.random.fold_in(_gk, 2), (25000,), 0, 3125, jnp.int32)
        _d = jax.random.randint(jax.random.fold_in(_gk, 3), (25000,), 0, 3125, jnp.int32)
        _loop = jnp.arange(3125, dtype=jnp.int32)
        src = jnp.concatenate([_s, _d, _loop])
        dst = jnp.concatenate([_d, _s, _loop])
        _o = jnp.argsort(dst, stable=True)
        src = src[_o]
        dst = dst[_o]
        edge_attr_32 = 0.000196303 + 1.00016 * jax.random.normal(jax.random.fold_in(_gk, 11), (53125, 32), jnp.float32)
        return (x, src, dst, edge_attr_32)
    x, src, dst, edge_attr_32 = _rec_inputs()

    def _L0_gnn_setup():
        import jax, jax.numpy as jnp
        import numpy as np
        N_NODES = 50000
        DEGREE = 16
        N_EDGES = N_NODES * DEGREE
        D_FEAT = 96

        def _make_edge_index():
            dst = jnp.repeat(jnp.arange(N_NODES, dtype=jnp.int64), DEGREE)
            off = jnp.tile(jnp.arange(1, DEGREE + 1, dtype=jnp.int64), N_NODES)
            src = (dst + off) % N_NODES
            return jnp.stack([src, dst], axis=0)
        key = jax.random.key(seed)
        kx, kw, kb = jax.random.split(key, 3)
        x = jax.random.normal(kx, (N_NODES, D_FEAT), dtype=jnp.float32)
        W = jax.random.normal(kw, (D_FEAT, D_FEAT), dtype=jnp.float32) * (1.0 / np.sqrt(D_FEAT))
        B = jax.random.normal(kb, (D_FEAT, D_FEAT), dtype=jnp.float32) * (1.0 / np.sqrt(D_FEAT))
        edge_index = _make_edge_index()
        return {'x': x, 'edge_index': edge_index, 'W': W, 'B': B}
    _L0_gnn_all = _L0_gnn_setup()
    _L0_gnn_in = {k: v for k, v in _L0_gnn_all.items() if k in ('W', 'B')}
    del _L0_gnn_all

    def _L1_gnn_setup():
        import jax, jax.numpy as jnp
        import numpy as np
        N_NODES = 50000
        N_EDGES = 25000
        IN_DIM = 96
        OUT_DIM = 96
        EDGE_DIM = 32
        BN_EPS = 1e-05
        key = jax.random.key(seed)
        ks = jax.random.split(key, 12)
        x = jax.random.normal(ks[0], (N_NODES, IN_DIM), dtype=jnp.float32)
        edge_index = jax.random.randint(ks[1], (2, N_EDGES), 0, N_NODES, dtype=jnp.int64)
        edge_attr = jax.random.normal(ks[2], (N_EDGES, EDGE_DIM), dtype=jnp.float32)
        We = jax.random.normal(ks[3], (EDGE_DIM, IN_DIM), dtype=jnp.float32) / np.sqrt(EDGE_DIM)
        be = jnp.zeros((IN_DIM,), dtype=jnp.float32)
        W1 = jax.random.normal(ks[4], (IN_DIM, OUT_DIM), dtype=jnp.float32) / np.sqrt(IN_DIM)
        b1 = jnp.zeros((OUT_DIM,), dtype=jnp.float32)
        W2 = jax.random.normal(ks[5], (OUT_DIM, OUT_DIM), dtype=jnp.float32) / np.sqrt(OUT_DIM)
        b2 = jnp.zeros((OUT_DIM,), dtype=jnp.float32)
        gamma = jnp.ones((OUT_DIM,), dtype=jnp.float32)
        beta = jnp.zeros((OUT_DIM,), dtype=jnp.float32)
        return {'x': x, 'edge_index': edge_index, 'edge_attr': edge_attr, 'We': We, 'be': be, 'W1': W1, 'b1': b1, 'W2': W2, 'b2': b2, 'gamma': gamma, 'beta': beta}
    _L1_gnn_all = _L1_gnn_setup()
    _L1_gnn_in = {k: v for k, v in _L1_gnn_all.items() if k in ('We', 'be', 'W1', 'b1', 'W2', 'b2', 'gamma', 'beta')}
    del _L1_gnn_all
    return {'x': x, 'src': src, 'dst': dst, 'edge_attr_32': edge_attr_32, 'L0_gnn_W': _L0_gnn_in['W'], 'L0_gnn_B': _L0_gnn_in['B'], 'L1_gnn_We': _L1_gnn_in['We'], 'L1_gnn_be': _L1_gnn_in['be'], 'L1_gnn_W1': _L1_gnn_in['W1'], 'L1_gnn_b1': _L1_gnn_in['b1'], 'L1_gnn_W2': _L1_gnn_in['W2'], 'L1_gnn_b2': _L1_gnn_in['b2'], 'L1_gnn_gamma': _L1_gnn_in['gamma'], 'L1_gnn_beta': _L1_gnn_in['beta']}

def reference(x, src, dst, edge_attr_32, L0_gnn_W, L0_gnn_B, L1_gnn_We, L1_gnn_be, L1_gnn_W1, L1_gnn_b1, L1_gnn_W2, L1_gnn_b2, L1_gnn_gamma, L1_gnn_beta):
    import jax
    import jax.numpy as jnp

    def _L0_gnn_ref(x, edge_index, W, B):
        import jax, jax.numpy as jnp
        import numpy as np
        N_NODES = 50000
        DEGREE = 16
        N_EDGES = N_NODES * DEGREE
        D_FEAT = 96

        def _make_edge_index():
            dst = jnp.repeat(jnp.arange(N_NODES, dtype=jnp.int64), DEGREE)
            off = jnp.tile(jnp.arange(1, DEGREE + 1, dtype=jnp.int64), N_NODES)
            src = (dst + off) % N_NODES
            return jnp.stack([src, dst], axis=0)
        num_nodes = x.shape[0]
        src, dst = (edge_index[0], edge_index[1])
        msg = x[src]
        agg = jax.ops.segment_sum(msg, dst, num_segments=num_nodes)
        deg = jax.ops.segment_sum(jnp.ones(src.shape[0], dtype=x.dtype), dst, num_segments=num_nodes)
        deg = jnp.where(deg == 0, jnp.ones_like(deg), deg)
        neighbor_term = agg / deg[:, None] @ W.T
        self_term = x @ B.T
        return neighbor_term + self_term

    def _L1_gnn_ref(x, edge_index, edge_attr, We, be, W1, b1, W2, b2, gamma, beta):
        import jax, jax.numpy as jnp
        import numpy as np
        N_NODES = 50000
        N_EDGES = 25000
        IN_DIM = 96
        OUT_DIM = 96
        EDGE_DIM = 32
        BN_EPS = 1e-05
        src = edge_index[0]
        dst = edge_index[1]
        msg = jax.nn.relu(x[src] + edge_attr @ We + be)
        aggr = jax.ops.segment_sum(msg, dst, num_segments=x.shape[0])
        h = x + aggr
        h = jax.nn.relu(h @ W1 + b1) @ W2 + b2
        mean = jnp.mean(h, axis=0)
        var = jnp.mean(jnp.square(h - mean), axis=0)
        h = (h - mean) * jax.lax.rsqrt(var + BN_EPS) * gamma + beta
        return jax.nn.relu(h)
    edge_index = jnp.stack([src, dst])
    h = jnp.maximum(_layernorm(x, axis=-1), 0.0)
    x = x + _L0_gnn_ref(h, edge_index, L0_gnn_W, L0_gnn_B)
    h = jnp.maximum(_layernorm(x, axis=-1), 0.0)
    x = x + _L1_gnn_ref(h, edge_index, edge_attr_32, L1_gnn_We, L1_gnn_be, L1_gnn_W1, L1_gnn_b1, L1_gnn_W2, L1_gnn_b2, L1_gnn_gamma, L1_gnn_beta)
    return x

_drawn_inputs = setup_inputs


def setup_inputs(seed=0):
    import zlib

    import numpy as np

    out = dict(_drawn_inputs(seed))
    spreads = {'L1_gnn_be': (0.0, 0.1),
     'L1_gnn_b1': (0.0, 2.0),
     'L1_gnn_b2': (0.0, 2.0),
     'L1_gnn_gamma': (1.0, 0.2),
     'L1_gnn_beta': (0.0, 0.1)}
    factors = {}
    for name, (base, spread) in spreads.items():
        noise = np.random.default_rng([zlib.crc32(name.encode()), seed]).standard_normal(out[name].shape)
        drawn = base * np.exp(spread * noise) if base else spread * noise
        out[name] = jnp.asarray(drawn.astype(out[name].dtype))
    for name, factor in factors.items():
        out[name] = (out[name] * factor).astype(out[name].dtype)
    return out
```

```python
import concourse.bass as bass
from concourse import mybir
from contextlib import ExitStack

N_NODES = 3125
FEAT = 96
EDGE_FEAT = 32
N_EDGES = 53125

TILE = 128
TILES_PER_GROUP = 8
GROUP = TILE * TILES_PER_GROUP
N_GROUPS = -(-N_EDGES // GROUP)
N_TILES = N_GROUPS * TILES_PER_GROUP
PADDED_EDGES = N_TILES * TILE
LAST_TILE = (N_EDGES - 1) // TILE
LAST_ROWS = N_EDGES - LAST_TILE * TILE
SLOTS = 4
ROUNDS = N_GROUPS // SLOTS
WINDOW = 128
N_WINDOWS = -(-N_NODES // WINDOW)

PARTS = 125
BLOCKS = N_NODES // PARTS
ROW = FEAT + 1
BANK = 512
BLOCKS_T = BANK // PARTS
CHUNKS_T = [(b, min(b + BLOCKS_T, BLOCKS)) for b in range(0, BLOCKS, BLOCKS_T)]
BLOCKS_N = BANK // ROW
CHUNKS_N = [(b, min(b + BLOCKS_N, BLOCKS)) for b in range(0, BLOCKS, BLOCKS_N)]
EPS = 1e-5

assert N_GROUPS == SLOTS * ROUNDS and BLOCKS * PARTS == N_NODES
assert LAST_TILE == N_TILES - 1 and len(CHUNKS_T) == 7 and len(CHUNKS_N) == 5


def gnn_two_layers(nc, x, src, dst, dst_grouped, edge_attr, w_neigh, w_self, w_edge, b_edge,
                   w1, b1, w2, b2, gamma, beta, out):
    fp32 = mybir.dt.float32
    i32 = mybir.dt.int32
    ALU = mybir.AluOpType
    ACT = mybir.ActivationFunctionType
    AX = mybir.AxisListType.X

    tables = [nc.dram_tensor(f"feature_table{layer}", (N_NODES, FEAT), fp32, kind="Internal").ap()
              for layer in range(2)]

    with ExitStack() as ctx:
        def sb(name, shape, dt=fp32):
            return ctx.enter_context(nc.sbuf_tensor(name, shape, dt))

        def sem(name):
            return ctx.enter_context(nc.semaphore(name))

        x_sb = sb("x_sb", [PARTS, BLOCKS, FEAT])
        x_self = sb("x_self", [PARTS, BLOCKS, FEAT])
        h = sb("h", [PARTS, BLOCKS, FEAT])
        scratch = sb("scratch", [PARTS, BLOCKS, FEAT])
        mean = sb("mean", [PARTS, BLOCKS])
        var = sb("var", [PARTS, BLOCKS])
        rstd = sb("rstd", [PARTS, BLOCKS])
        degree = sb("degree", [PARTS, BLOCKS])
        hT = sb("hT", [FEAT, BLOCKS, PARTS])
        r1T = sb("r1T", [FEAT, BLOCKS, PARTS])
        h2T = sb("h2T", [FEAT, BLOCKS, PARTS])
        sums = [sb(f"sums{layer}", [ROW, N_NODES + WINDOW]) for layer in range(2)]

        src_idx = sb("src_idx", [TILE, N_TILES + SLOTS * TILES_PER_GROUP], i32)
        slot_idx = sb("slot_idx", [TILE, SLOTS, TILES_PER_GROUP], i32)
        dst_i = sb("dst_i", [TILE, N_TILES], i32)
        dst_f = sb("dst_f", [TILE, N_TILES])
        dst_rel = sb("dst_rel", [TILE, N_TILES])
        grp_i = sb("grp_i", [N_GROUPS, GROUP], i32)
        grp_f = sb("grp_f", [N_GROUPS, GROUP])
        grp_min = sb("grp_min", [N_GROUPS, 1])
        grp_max = sb("grp_max", [N_GROUPS, 1])
        grp_wide = sb("grp_wide", [N_GROUPS, 1])
        grp_diag = sb("grp_diag", [N_GROUPS, N_GROUPS])
        starts_i = sb("starts_i", [1, N_GROUPS], i32)
        wide_i = sb("wide_i", [1, 1], i32)
        iota_i = sb("iota_i", [TILE, N_WINDOWS * WINDOW], i32)
        iota_f = sb("iota_f", [TILE, N_WINDOWS * WINDOW])
        part_i = sb("part_i", [TILE, 1], i32)
        part_f = sb("part_f", [TILE, 1])
        identity = sb("identity", [TILE, TILE])
        ones = sb("ones", [TILE, TILE])

        rows = sb("rows", [TILE, SLOTS, TILES_PER_GROUP, ROW])
        onehot = sb("onehot", [TILE, TILES_PER_GROUP, WINDOW])
        message = sb("message", [TILE, TILES_PER_GROUP, FEAT])
        edges = sb("edges", [EDGE_FEAT + 1, SLOTS, GROUP])
        pool_in = sb("pool_in", [1, 1], i32)
        pool_out = sb("pool_out", [1, 1], i32)

        w_neigh_sb = sb("w_neigh_sb", [ROW, ROW])
        w_self_sb = sb("w_self_sb", [FEAT, FEAT])
        w_edge_sb = sb("w_edge_sb", [EDGE_FEAT + 1, FEAT])
        w1_sb = sb("w1_sb", [FEAT, FEAT])
        w2_sb = sb("w2_sb", [FEAT, FEAT])
        columns = sb("columns", [FEAT, 4])
        bn_parts = sb("bn_parts", [FEAT, len(CHUNKS_T), 6])
        bn = sb("bn", [FEAT, 2])
        bn_scale = sb("bn_scale", [FEAT, 1])
        bn_shift = sb("bn_shift", [FEAT, 1])
        eps_col = sb("eps_col", [TILE, 1])

        psum = ctx.enter_context(nc.psum_tensor("psum", [TILE, 8, BANK], fp32))
        win_ps = psum[0:ROW, 0, 0:WINDOW]
        edge_ps = [psum[:, 1 + half, 0:BANK * 3 // 4] for half in range(2)]

        def transposed_ps(c):
            b0, b1_ = CHUNKS_T[c]
            return psum[0:FEAT, 1 + c, 0:(b1_ - b0) * PARTS]

        def node_ps(c, width):
            b0, b1_ = CHUNKS_N[c]
            return psum[0:PARTS, 3 + c, 0:(b1_ - b0) * width].rearrange("p (b f) -> p b f", f=width)

        def per_block(stat, b0=0, b1_=BLOCKS):
            return stat[:, b0:b1_].rearrange("p (b o) -> p b o", o=1).to_broadcast([PARTS, b1_ - b0, FEAT])

        x_loaded = sem("x_loaded")
        src_loaded = sem("src_loaded")
        dst_loaded = sem("dst_loaded")
        grp_loaded = sem("grp_loaded")
        weights_loaded = sem("weights_loaded")
        edges_loaded = [sem(f"edges_loaded{k}") for k in range(SLOTS)]
        gathered = [sem(f"gathered{k}") for k in range(SLOTS)]
        iota_made = sem("iota_made")
        consts_made = sem("consts_made")
        dve_step = sem("dve_step")
        gate_passed = sem("gate_passed")
        slot_ready = sem("slot_ready")
        centred = sem("centred")
        squared = sem("squared")
        var_ready = sem("var_ready")
        std_ready = sem("std_ready")
        h_ready = sem("h_ready")
        table_written = sem("table_written")
        transposed = sem("transposed")
        hT_copied = sem("hT_copied")
        self_done = sem("self_done")
        self_added = sem("self_added")
        diag_ready = sem("diag_ready")
        starts_done = sem("starts_done")
        routing_ready = sem("routing_ready")
        onehot_ready = sem("onehot_ready")
        scattered = sem("scattered")
        pass_onehot = sem("pass_onehot")
        pass_scattered = sem("pass_scattered")
        sums_done = sem("sums_done")
        neigh_done = sem("neigh_done")
        edge_terms = sem("edge_terms")
        summed = sem("summed")
        message_ready = sem("message_ready")
        hT_summed = sem("hT_summed")
        mm1_done = sem("mm1_done")
        r1_ready = sem("r1_ready")
        mm2_done = sem("mm2_done")
        bn_var = sem("bn_var")
        bn_std = sem("bn_std")
        bn_ready = sem("bn_ready")
        resultT_ready = sem("resultT_ready")
        result_done = sem("result_done")
        out_ready = sem("out_ready")
        out_written = sem("out_written")

        b1_col, b2_col, gamma_col, beta_col = (columns[:, i:i + 1] for i in range(4))

        block = ctx.enter_context(nc.Block())

        @block.sync
        def _(sp):
            for p0, p1 in ((0, 112), (112, PARTS)):
                sp.dma_start(x_sb[p0:p1], x.rearrange("(p b) f -> p b f", b=BLOCKS)[p0:p1]).then_inc(x_loaded, 16)
            sp.dma_start(src_idx[:, 0:N_TILES], src).then_inc(src_loaded, 16)
            sp.dma_start(src_idx[:, N_TILES:], src[:, 0:SLOTS * TILES_PER_GROUP]).then_inc(src_loaded, 16)
            sp.dma_start(dst_i[:], dst).then_inc(dst_loaded, 16)
            sp.dma_start(grp_i[:], dst_grouped).then_inc(grp_loaded, 16)
            sp.wait_ge(consts_made, 1)
            sp.dma_start(w_neigh_sb[0:FEAT, 0:FEAT], w_neigh).then_inc(weights_loaded, 16)
            for dst_ap, src_ap in ((w_self_sb[:], w_self), (w_edge_sb[0:EDGE_FEAT], w_edge),
                                   (w_edge_sb[EDGE_FEAT:], b_edge), (w1_sb[:], w1), (w2_sb[:], w2),
                                   (b1_col, b1), (b2_col, b2), (gamma_col, gamma), (beta_col, beta)):
                sp.dma_start(dst_ap, src_ap).then_inc(weights_loaded, 16)
            sp.wait_ge(h_ready, 1)
            for p0, p1 in ((0, 112), (112, PARTS)):
                sp.dma_start(tables[0].rearrange("(p b) f -> p b f", b=BLOCKS)[p0:p1],
                             h[p0:p1]).then_inc(table_written, 16)
            for k in range(SLOTS):
                sp.dma_start(edges[0:EDGE_FEAT, k, :], edge_attr[k]).then_inc(edges_loaded[k], 16)
            sp.wait_ge(h_ready, 2)
            for p0, p1 in ((0, 112), (112, PARTS)):
                sp.dma_start(tables[1].rearrange("(p b) f -> p b f", b=BLOCKS)[p0:p1],
                             h[p0:p1]).then_inc(table_written, 16)
            with sp.Fori(1, ROUNDS) as r:
                for k in range(SLOTS):
                    sp.wait_ge(edge_terms, (r - 1) * SLOTS + k + 1)
                    sp.dma_start(edges[0:EDGE_FEAT, k, :],
                                 edge_attr[bass.ds(r * SLOTS + k, 1)].rearrange("g f e -> (g f) e")
                                 ).then_inc(edges_loaded[k], 16)
            for half, (p0, p1) in enumerate(((0, 112), (112, PARTS))):
                sp.wait_ge(out_ready, 1)
                sp.dma_start(out.rearrange("(p b) f -> p b f", b=BLOCKS)[p0:p1],
                             x_self[p0:p1]).then_inc(out_written, 16)
            sp.wait_ge(table_written, 64)
            sp.wait_ge(out_written, 32)

        @block.gpsimd
        def _(pool):
            nc.gpsimd.iota(iota_i[:], pattern=[[1, N_WINDOWS * WINDOW]], base=0,
                           channel_multiplier=0).then_inc(iota_made, 1)
            nc.gpsimd.iota(part_i[:], pattern=[[0, 1]], base=0, channel_multiplier=1).then_inc(iota_made, 1)
            nc.gpsimd.memset(pool_in[:], 0).then_inc(gate_passed, 1)
            for layer in range(2):
                pool.wait_ge(table_written, 32 * (layer + 1))
                with pool.Fori(0, ROUNDS) as r:
                    for k in range(SLOTS):
                        if k % 2 == 0:
                            pool.wait_ge(gate_passed, (layer * N_GROUPS + r * SLOTS + k) // 2 + 1)
                            pool.wait_ge(slot_ready, layer * N_GROUPS + r * SLOTS + k + 2)
                            nc.gpsimd.tensor_tensor(pool_out[:], pool_in[:], pool_in[:], ALU.add).then_inc(gate_passed, 1)
                        for j in range(TILES_PER_GROUP):
                            nc.gpsimd.indirect_dma_start(
                                out=rows[:, k, j, 0:FEAT], out_offset=None, in_=tables[layer],
                                in_offset=bass.IndirectOffsetOnAxis(ap=slot_idx[:, k, j:j + 1], axis=0),
                            ).then_inc(gathered[k], 16)

        @block.vector
        def _(dve):
            steps = [0]

            def chained(instruction):
                steps[0] += 1
                instruction.then_inc(dve_step, 1)
                dve.wait_ge(dve_step, steps[0])

            nc.vector.memset(w_neigh_sb[:], 0.0)
            chained(nc.vector.memset(ones[:], 1.0))
            nc.vector.memset(w_neigh_sb[FEAT:ROW, FEAT:ROW], 1.0).then_inc(consts_made, 1)
            nc.vector.memset(edges[EDGE_FEAT:, :, :], 1.0)
            nc.vector.memset(eps_col[:], EPS)
            nc.vector.memset(rows[:, :, :, FEAT:ROW], 1.0)
            nc.vector.memset(sums[0][:], 0.0)
            nc.vector.memset(sums[1][:], 0.0)

            def layernorm(features, layer):
                chained(nc.vector.tensor_reduce(mean[:], features, AX, ALU.add))
                chained(nc.vector.tensor_scalar(mean[:], mean[:], 1.0 / FEAT, None, ALU.mult))
                nc.vector.tensor_tensor(h[:], features, per_block(mean), ALU.subtract).then_inc(centred, 1)
                dve.wait_ge(squared, layer + 1)
                nc.vector.tensor_reduce(var[:], scratch[:], AX, ALU.add).then_inc(var_ready, 1)
                dve.wait_ge(std_ready, layer + 1)
                chained(nc.vector.reciprocal(rstd[:], rstd[:]))
                nc.vector.tensor_scalar(h[:], h[:], 0.0, None, ALU.max)
                steps[0] += 1
                nc.vector.drain().then_inc(dve_step, 1)
                dve.wait_ge(dve_step, steps[0])
                nc.vector.tensor_tensor(h[:], h[:], per_block(rstd), ALU.mult).then_inc(h_ready, 1)

            dve.wait_ge(x_loaded, 32)
            layernorm(x_sb[:], 0)

            dve.wait_ge(src_loaded, 32)
            nc.vector.tensor_copy(slot_idx[:].rearrange("p s t -> p (s t)"),
                                  src_idx[:, 0:SLOTS * TILES_PER_GROUP]).then_inc(slot_ready, SLOTS)

            dve.wait_ge(iota_made, 2)
            nc.vector.tensor_copy(part_f[:], part_i[:])
            chained(nc.vector.tensor_copy(iota_f[:], iota_i[:]))
            nc.vector.tensor_scalar(identity[:], iota_f[:, 0:TILE], part_f[:], None,
                                    ALU.is_equal).then_inc(consts_made, 1)

            dve.wait_ge(grp_loaded, 16)
            chained(nc.vector.tensor_copy(grp_f[:], grp_i[:]))
            nc.vector.tensor_reduce(grp_min[:], grp_f[:], AX, ALU.min)
            chained(nc.vector.tensor_reduce(grp_max[:], grp_f[:], AX, ALU.max))
            chained(nc.vector.tensor_tensor(grp_wide[:], grp_max[:], grp_min[:], ALU.subtract))
            chained(nc.vector.tensor_scalar(grp_wide[:], grp_wide[:], float(WINDOW), None, ALU.is_ge))
            nc.vector.tensor_scalar(grp_diag[:], identity[0:N_GROUPS, 0:N_GROUPS], grp_min[:], None,
                                    ALU.mult).then_inc(diag_ready, 1)

            dve.wait_ge(dst_loaded, 16)
            chained(nc.vector.tensor_copy(dst_f[:], dst_i[:]))
            chained(nc.vector.memset(dst_f[:, LAST_TILE:], -1e6))
            chained(nc.vector.tensor_copy(dst_f[0:LAST_ROWS, LAST_TILE:], dst_i[0:LAST_ROWS, LAST_TILE:]))
            dve.wait_ge(starts_done, 1)
            nc.vector.tensor_tensor(
                dst_rel[:].rearrange("p (g t) -> p g t", t=TILES_PER_GROUP),
                dst_f[:].rearrange("p (g t) -> p g t", t=TILES_PER_GROUP),
                psum[:, 0, 0:N_GROUPS].rearrange("p (g o) -> p g o", o=1).to_broadcast(
                    [TILE, N_GROUPS, TILES_PER_GROUP]), ALU.subtract)
            nc.vector.tensor_copy(starts_i[:], psum[0:1, 0, 0:N_GROUPS])
            chained(nc.vector.tensor_copy(wide_i[:], psum[0:1, 0, N_GROUPS:N_GROUPS + 1]))
            nc.vector.drain().then_inc(routing_ready, 1)

            for c, (b0, b1_) in enumerate(CHUNKS_N):
                dve.wait_ge(self_done, c + 1)
                nc.vector.tensor_tensor(x_self[:, b0:b1_], x_sb[:, b0:b1_], node_ps(c, FEAT),
                                        ALU.add).then_inc(self_added, 1)

            def make_onehot(dst_of_edge, node_columns):
                return nc.vector.tensor_tensor(
                    onehot[:],
                    node_columns.rearrange("p (o n) -> p o n", o=1).to_broadcast([TILE, TILES_PER_GROUP, WINDOW]),
                    dst_of_edge.rearrange("p (t o) -> p t o", o=1).to_broadcast([TILE, TILES_PER_GROUP, WINDOW]),
                    ALU.is_equal)

            def add_edge_terms(group, k, r):
                dve.wait_ge(gathered[k], (ROUNDS + r + 1) * 16 * TILES_PER_GROUP)
                dve.wait_ge(edge_terms, group + 1)
                half_tiles = TILES_PER_GROUP // 2
                for half in range(2):
                    tiles = slice(half * half_tiles, (half + 1) * half_tiles)
                    last = nc.vector.tensor_tensor(
                        message[:, tiles], rows[:, k, tiles, 0:FEAT],
                        edge_ps[half].rearrange("p (t f) -> p t f", f=FEAT), ALU.add)
                last.then_inc(summed, 1)

            def refill_slot(k, group):
                nc.vector.tensor_copy(
                    slot_idx[:, k, :],
                    src_idx[:, bass.ds((group + SLOTS) * TILES_PER_GROUP, TILES_PER_GROUP)]
                ).then_inc(slot_ready, 1)

            def scatter_layer(layer, general):
                with dve.Fori(0, ROUNDS) as r:
                    for k in range(SLOTS):
                        group = r * SLOTS + k
                        group_dst = bass.ds(group * TILES_PER_GROUP, TILES_PER_GROUP)
                        if not general:
                            start = dve.value_load(starts_i[0:1, bass.ds(group, 1)],
                                                   min_val=0, max_val=N_NODES - 1)
                            make_onehot(dst_rel[:, group_dst], iota_f[:, 0:WINDOW]).then_inc(onehot_ready, 1)
                            if layer == 1:
                                add_edge_terms(group, k, r)
                            dve.wait_ge(scattered, layer * N_GROUPS + group + 1)
                            window = sums[layer][:, bass.ds(start, WINDOW)]
                            nc.vector.tensor_tensor(window, window, win_ps, ALU.add)
                        else:
                            if layer == 1:
                                add_edge_terms(group, k, r)
                            with dve.Fori(0, N_WINDOWS) as w:
                                passes = (layer * N_GROUPS + group) * N_WINDOWS + w
                                make_onehot(dst_f[:, group_dst],
                                            iota_f[:, bass.ds(w * WINDOW, WINDOW)]).then_inc(pass_onehot, 1)
                                dve.wait_ge(pass_scattered, passes + 1)
                                window = sums[layer][:, bass.ds(w * WINDOW, WINDOW)]
                                nc.vector.tensor_tensor(window, window, win_ps, ALU.add)
                        refill_slot(k, group)

            wide = dve.value_load(wide_i[0:1, 0:1], min_val=0, max_val=N_GROUPS)

            def scatter_either(layer):
                with dve.If(wide):
                    scatter_layer(layer, general=True)
                with dve.Else():
                    scatter_layer(layer, general=False)
                nc.vector.drain().then_inc(sums_done, 1)

            scatter_either(0)

            for c, (b0, b1_) in enumerate(CHUNKS_N):
                dve.wait_ge(neigh_done, c + 1)
                chained(nc.vector.tensor_scalar(degree[:, b0:b1_], node_ps(c, ROW)[:, :, FEAT], 1.0, None, ALU.max))
                chained(nc.vector.reciprocal(degree[:, b0:b1_], degree[:, b0:b1_]))
                chained(nc.vector.tensor_tensor(scratch[:, b0:b1_], node_ps(c, ROW)[:, :, 0:FEAT],
                                                per_block(degree, b0, b1_), ALU.mult))
                nc.vector.tensor_tensor(x_self[:, b0:b1_], x_self[:, b0:b1_], scratch[:, b0:b1_], ALU.add)
            steps[0] += 1
            nc.vector.drain().then_inc(dve_step, 1)
            dve.wait_ge(dve_step, steps[0])
            dve.wait_ge(table_written, 32)
            layernorm(x_self[:], 1)

            scatter_either(1)

            dve.wait_ge(hT_copied, 2 * len(CHUNKS_T))
            node_order = sums[1][0:FEAT, 0:N_NODES].rearrange("f (p b) -> f b p", b=BLOCKS)
            for b0, b1_ in CHUNKS_T:
                nc.vector.tensor_tensor(hT[:, b0:b1_], hT[:, b0:b1_], node_order[:, b0:b1_],
                                        ALU.add).then_inc(hT_summed, 1)
            dve.wait_ge(weights_loaded, 160)
            for c, (b0, b1_) in enumerate(CHUNKS_T):
                dve.wait_ge(mm2_done, c + 1)
                cols = h2T[:, b0:b1_].rearrange("f b p -> f (b p)")
                chained(nc.vector.tensor_scalar(cols, psum[0:FEAT, c, 0:(b1_ - b0) * PARTS], b2_col, None, ALU.add))
                last = nc.vector.bn_stats(bn_parts[:, c, :], cols)
            chained(last)
            nc.vector.bn_aggr(bn[:], bn_parts[:].rearrange("f c s -> f (c s)")).then_inc(bn_var, 1)
            dve.wait_ge(bn_std, 1)
            chained(nc.vector.reciprocal(bn_scale[:], bn_scale[:]))
            chained(nc.vector.tensor_tensor(bn_scale[:], bn_scale[:], gamma_col, ALU.mult))
            chained(nc.vector.tensor_tensor(bn_shift[:], bn[:, 0:1], bn_scale[:], ALU.mult))
            nc.vector.tensor_tensor(bn_shift[:], beta_col, bn_shift[:], ALU.subtract).then_inc(bn_ready, 1)
            for c, (b0, b1_) in enumerate(CHUNKS_N):
                dve.wait_ge(result_done, c + 1)
                last = nc.vector.tensor_tensor(x_self[:, b0:b1_], x_self[:, b0:b1_], node_ps(c, FEAT), ALU.add)
            last.then_inc(out_ready, 1)

        @block.scalar
        def _(act):
            def layernorm_parts(layer):
                act.wait_ge(centred, layer + 1)
                nc.scalar.activation(scratch[:], h[:], ACT.Square).then_inc(squared, 1)
                act.wait_ge(var_ready, layer + 1)
                nc.scalar.activation(rstd[:], var[:], ACT.Sqrt, bias=eps_col[0:PARTS],
                                     scale=1.0 / FEAT).then_inc(std_ready, 1)

            def copy_transposed(layer):
                for c, (b0, b1_) in enumerate(CHUNKS_T):
                    act.wait_ge(transposed, layer * len(CHUNKS_T) + c + 1)
                    if layer == 1 and c == 0:
                        act.wait_ge(self_done, len(CHUNKS_N))
                    nc.scalar.copy(hT[:, b0:b1_].rearrange("f b p -> f (b p)"),
                                   transposed_ps(c)).then_inc(hT_copied, 1)

            layernorm_parts(0)
            copy_transposed(0)
            layernorm_parts(1)
            copy_transposed(1)
            with act.Fori(0, N_GROUPS) as group:
                act.wait_ge(summed, group + 1)
                nc.scalar.activation(message[:], message[:], ACT.Relu).then_inc(message_ready, 1)
            act.wait_ge(weights_loaded, 160)
            for c, (b0, b1_) in enumerate(CHUNKS_T):
                act.wait_ge(mm1_done, c + 1)
                nc.scalar.activation(r1T[:, b0:b1_].rearrange("f b p -> f (b p)"), transposed_ps(c), ACT.Relu,
                                     bias=b1_col).then_inc(r1_ready, 1)
            act.wait_ge(bn_var, 1)
            nc.scalar.activation(bn_scale[:], bn[:, 1:2], ACT.Sqrt, bias=eps_col[0:FEAT]).then_inc(bn_std, 1)
            act.wait_ge(bn_ready, 1)
            for b0, b1_ in CHUNKS_N:
                nc.scalar.activation(r1T[:, b0:b1_], h2T[:, b0:b1_], ACT.Relu, bias=bn_shift[:],
                                     scale=bn_scale[:]).then_inc(resultT_ready, 1)

        @block.tensor
        def _(pe):
            def transpose_h(layer):
                pe.wait_ge(h_ready, layer + 1)
                for c, (b0, b1_) in enumerate(CHUNKS_T):
                    for b in range(b0, b1_):
                        last = nc.tensor.transpose(
                            transposed_ps(c)[:, (b - b0) * PARTS:(b - b0 + 1) * PARTS], h[:, b, :],
                            identity[0:PARTS, 0:PARTS])
                    last.then_inc(transposed, 1)

            pe.wait_ge(consts_made, 2)
            pe.wait_ge(diag_ready, 1)
            nc.tensor.matmul(psum[:, 0, 0:N_GROUPS], ones[0:N_GROUPS, :], grp_diag[:], start=True, stop=True)
            nc.tensor.matmul(psum[:, 0, N_GROUPS:N_GROUPS + 1], ones[0:N_GROUPS, :], grp_wide[:],
                             start=True, stop=True).then_inc(starts_done, 1)
            transpose_h(0)

            pe.wait_ge(weights_loaded, 160)
            pe.wait_ge(hT_copied, len(CHUNKS_T))
            for c, (b0, b1_) in enumerate(CHUNKS_N):
                for b in range(b0, b1_):
                    last = nc.tensor.matmul(node_ps(c, FEAT)[:, b - b0, :], hT[:, b, :], w_self_sb[:],
                                            start=True, stop=True)
                last.then_inc(self_done, 1)

            def scatter(width, lhs, counter):
                for j in range(TILES_PER_GROUP):
                    last = nc.tensor.matmul(psum[0:width, 0, 0:WINDOW], lhs(j), onehot[:, j, :],
                                            start=(j == 0), stop=(j == TILES_PER_GROUP - 1))
                last.then_inc(counter, 1)

            def scatter_layer(layer, general):
                with pe.Fori(0, ROUNDS) as r:
                    for k in range(SLOTS):
                        group = r * SLOTS + k
                        if layer == 0:
                            width, lhs = ROW, lambda j, k=k: rows[:, k, j, :]
                            lhs_there = (gathered[k], (r + 1) * 16 * TILES_PER_GROUP)
                        else:
                            width, lhs = FEAT, lambda j: message[:, j, :]
                            pe.wait_ge(edges_loaded[k], (r + 1) * 16)
                            for j in range(TILES_PER_GROUP):
                                half, place = divmod(j, TILES_PER_GROUP // 2)
                                last = nc.tensor.matmul(edge_ps[half][:, place * FEAT:(place + 1) * FEAT],
                                                        edges[:, k, j * TILE:(j + 1) * TILE], w_edge_sb[:],
                                                        start=True, stop=True)
                                if j == TILES_PER_GROUP - 1:
                                    last.then_inc(edge_terms, 1)
                            lhs_there = (message_ready, group + 1)
                        if not general:
                            pe.wait_ge(*lhs_there)
                            pe.wait_ge(onehot_ready, layer * N_GROUPS + group + 1)
                            scatter(width, lhs, scattered)
                        else:
                            with pe.Fori(0, N_WINDOWS) as w:
                                pe.wait_ge(*lhs_there)
                                pe.wait_ge(pass_onehot, (layer * N_GROUPS + group) * N_WINDOWS + w + 1)
                                scatter(width, lhs, pass_scattered)

            wide = None

            def scatter_either(layer):
                with pe.If(wide):
                    scatter_layer(layer, general=True)
                with pe.Else():
                    scatter_layer(layer, general=False)

            pe.wait_ge(routing_ready, 1)
            wide = pe.value_load(wide_i[0:1, 0:1], min_val=0, max_val=N_GROUPS)
            pe.wait_ge(self_added, len(CHUNKS_N))
            scatter_either(0)

            pe.wait_ge(sums_done, 1)
            blocks = sums[0][:, 0:N_NODES].rearrange("f (p b) -> f b p", b=BLOCKS)
            for c, (b0, b1_) in enumerate(CHUNKS_N):
                for b in range(b0, b1_):
                    last = nc.tensor.matmul(node_ps(c, ROW)[:, b - b0, :], blocks[:, b, :], w_neigh_sb[:],
                                            start=True, stop=True)
                last.then_inc(neigh_done, 1)
            transpose_h(1)
            pe.wait_ge(hT_copied, 2 * len(CHUNKS_T))
            scatter_either(1)

            for c, (b0, b1_) in enumerate(CHUNKS_T):
                pe.wait_ge(hT_summed, c + 1)
                nc.tensor.matmul(transposed_ps(c), w1_sb[:], hT[:, b0:b1_].rearrange("f b p -> f (b p)"),
                                 start=True, stop=True).then_inc(mm1_done, 1)
            for c, (b0, b1_) in enumerate(CHUNKS_T):
                pe.wait_ge(r1_ready, c + 1)
                nc.tensor.matmul(psum[0:FEAT, c, 0:(b1_ - b0) * PARTS], w2_sb[:],
                                 r1T[:, b0:b1_].rearrange("f b p -> f (b p)"),
                                 start=True, stop=True).then_inc(mm2_done, 1)
            for c, (b0, b1_) in enumerate(CHUNKS_N):
                pe.wait_ge(resultT_ready, c + 1)
                for b in range(b0, b1_):
                    last = nc.tensor.transpose(node_ps(c, FEAT)[:, b - b0, :], r1T[:, b, :],
                                               identity[0:FEAT, 0:FEAT])
                last.then_inc(result_done, 1)


def kernel(x, src, dst, edge_attr_32, L0_gnn_W, L0_gnn_B, L1_gnn_We, L1_gnn_be, L1_gnn_W1, L1_gnn_b1,
           L1_gnn_W2, L1_gnn_b2, L1_gnn_gamma, L1_gnn_beta):
    import numpy as np
    import concourse.bacc as bacc
    from concourse.bass_utils import run_bass_kernel_spmd

    pad = PADDED_EDGES - N_EDGES
    src_p = np.pad(np.asarray(src), (0, pad))
    dst_p = np.pad(np.asarray(dst), (0, pad), mode="edge")
    edge_p = np.pad(np.asarray(edge_attr_32), ((0, pad), (0, 0)))
    arrays = {
        "x": np.asarray(x),
        "src": src_p.reshape(N_TILES, TILE).T,
        "dst": dst_p.reshape(N_TILES, TILE).T,
        "dst_grouped": dst_p.reshape(N_GROUPS, GROUP),
        "edge_attr": edge_p.reshape(N_GROUPS, GROUP, EDGE_FEAT).transpose(0, 2, 1),
        "w_neigh": np.asarray(L0_gnn_W).T,
        "w_self": np.asarray(L0_gnn_B).T,
        "w_edge": np.asarray(L1_gnn_We),
        "b_edge": np.asarray(L1_gnn_be).reshape(1, FEAT),
        "w1": np.asarray(L1_gnn_W1),
        "b1": np.asarray(L1_gnn_b1).reshape(FEAT, 1),
        "w2": np.asarray(L1_gnn_W2),
        "b2": np.asarray(L1_gnn_b2).reshape(FEAT, 1),
        "gamma": np.asarray(L1_gnn_gamma).reshape(FEAT, 1),
        "beta": np.asarray(L1_gnn_beta).reshape(FEAT, 1),
    }
    arrays = {name: np.ascontiguousarray(a) for name, a in arrays.items()}
    nc = bacc.Bacc("TRN2", target_bir_lowering=False, num_devices=1)
    args = [nc.dram_tensor(name, a.shape, mybir.dt.from_np(a.dtype), kind="ExternalInput").ap()
            for name, a in arrays.items()]
    out = nc.dram_tensor("out", (N_NODES, FEAT), mybir.dt.float32, kind="ExternalOutput").ap()
    gnn_two_layers(nc, *args, out)
    result = run_bass_kernel_spmd(nc, [arrays], core_ids=[0])
    return result.results[0]["out"]
```

```python
import concourse.bass as bass
from concourse import mybir
from contextlib import ExitStack

N_NODES = 3125
FEAT = 96
EDGE_FEAT = 32
N_EDGES = 53125

TILE = 128
TILES_PER_GROUP = 8
GROUP = TILE * TILES_PER_GROUP
N_GROUPS = -(-N_EDGES // GROUP)
N_TILES = N_GROUPS * TILES_PER_GROUP
PADDED_EDGES = N_TILES * TILE
LAST_TILE = (N_EDGES - 1) // TILE
LAST_ROWS = N_EDGES - LAST_TILE * TILE
SLOTS = 4
ROUNDS = N_GROUPS // SLOTS
WINDOW = 80
N_WINDOWS = -(-N_NODES // WINDOW)

DENSE_K = SLOTS - 1
SRC_BUFFERS = 4
SRC_PITCH = N_NODES + N_NODES % 2
SRC_SHIFT = N_NODES // 2
assert GROUP <= 2048 and SRC_SHIFT < 2048 and N_NODES - SRC_SHIFT < 2048

PARTS = 125
PART_SPANS = ((0, 112), (112, PARTS))
BLOCKS = N_NODES // PARTS
ROW = FEAT + 1
BANK = 512

CHUNK_BLOCKS = BANK // ROW
N_CHUNKS = BLOCKS // CHUNK_BLOCKS
CHUNK_NODES = CHUNK_BLOCKS * PARTS
ROUNDS_PER_CHUNK = 3
CHUNK_ROUNDS = [(c * ROUNDS_PER_CHUNK, min((c + 1) * ROUNDS_PER_CHUNK, ROUNDS)) for c in range(N_CHUNKS)]
HALVES = [(0, (CHUNK_BLOCKS + 1) // 2), ((CHUNK_BLOCKS + 1) // 2, CHUNK_BLOCKS)]
DVE_BLOCKS = 1
EPS = 1e-5

assert N_GROUPS == SLOTS * ROUNDS and BLOCKS * PARTS == N_NODES and LAST_TILE == N_TILES - 1
assert N_CHUNKS * CHUNK_BLOCKS == BLOCKS and CHUNK_ROUNDS[-1][1] == ROUNDS


def chunk_blocks(c):
    return slice(c * CHUNK_BLOCKS, (c + 1) * CHUNK_BLOCKS)


def gnn_two_layers(nc, x, src, dst, dst_grouped, edge_attr, w_neigh, w_self, w_edge, b_edge,
                   w1, b1, w2, b2, gamma, beta, out):
    fp32 = mybir.dt.float32
    i32 = mybir.dt.int32
    fp16 = mybir.dt.float16
    bf16 = mybir.dt.bfloat16
    ALU = mybir.AluOpType
    ACT = mybir.ActivationFunctionType
    AX = mybir.AxisListType.X

    tables = [nc.dram_tensor(f"feature_table{layer}", (N_NODES, FEAT), fp32, kind="Internal").ap()
              for layer in range(2)]

    def node_major(array):
        return array.rearrange("(b p) f -> p b f", p=PARTS)

    with ExitStack() as ctx:
        def sb(name, shape, dt=fp32):
            return ctx.enter_context(nc.sbuf_tensor(name, shape, dt))

        def sem(name):
            return ctx.enter_context(nc.semaphore(name))

        x_sb = sb("x_sb", [PARTS, BLOCKS, FEAT])
        x_mid = sb("x_mid", [PARTS, BLOCKS, FEAT])
        h = sb("h", [PARTS, BLOCKS, FEAT])
        block_stats = sb("block_stats", [PARTS, BLOCKS, 6])
        mean_var = sb("mean_var", [PARTS, BLOCKS, 2])
        rstd = sb("rstd", [PARTS, BLOCKS])
        neg_mean_rstd = sb("neg_mean_rstd", [PARTS, BLOCKS])
        degree = sb("degree", [PARTS, BLOCKS])
        hT = sb("hT", [FEAT, N_NODES])
        r1T = sb("r1T", [FEAT, N_NODES])
        h2T_space = sb("h2T_space", [TILE, N_NODES])
        h2T = h2T_space[0:FEAT]
        h_rest = h2T_space[0:PARTS, 0:BLOCKS * FEAT].rearrange("p (b f) -> p b f", f=FEAT)
        sums = [sb(f"sums{layer}", [ROW, N_NODES + WINDOW]) for layer in range(2)]

        src_idx = sb("src_idx", [TILE, N_TILES + SLOTS * TILES_PER_GROUP], i32)
        slot_idx = sb("slot_idx", [TILE, SLOTS, TILES_PER_GROUP], i32)
        dst_i = sb("dst_i", [TILE, N_TILES], i32)
        dst_f = sb("dst_f", [TILE, N_TILES])
        dst_rel = sb("dst_rel", [TILE, N_TILES])
        dst_pass = sb("dst_pass", [TILE, TILES_PER_GROUP])
        grp_i = sb("grp_i", [N_GROUPS, GROUP], i32)
        grp_min = sb("grp_min", [N_GROUPS, 1])
        grp_max = sb("grp_max", [N_GROUPS, 1])
        grp_odd = sb("grp_odd", [N_GROUPS, 4])
        grp_diag = sb("grp_diag", [N_GROUPS, N_GROUPS])
        starts_i = sb("starts_i", [1, N_GROUPS], i32)
        odd_i = sb("odd_i", [1, 1], i32)
        columns_i = sb("columns_i", [TILE, TILE], i32)
        columns_f = sb("columns_f", [TILE, TILE])
        windows_i = sb("windows_i", [TILE, N_WINDOWS], i32)
        windows_f = sb("windows_f", [TILE, N_WINDOWS])
        part_i = sb("part_i", [TILE, 1], i32)
        part_f = sb("part_f", [TILE, 1])
        identity = sb("identity", [TILE, TILE])
        ones = sb("ones", [N_GROUPS, TILE])

        rows = sb("rows", [TILE, SLOTS, TILES_PER_GROUP, ROW])
        onehot = [sb(f"onehot{i}", [TILE, TILES_PER_GROUP, WINDOW]) for i in range(2)]
        message = sb("message", [TILE, TILES_PER_GROUP, FEAT])
        edges = sb("edges", [EDGE_FEAT + 1, SLOTS, GROUP])
        src_f = sb("src_f", [TILE, N_TILES])
        src_numbers = sb("src_numbers", [TILE, SRC_PITCH], fp16)
        src_onehot = sb("src_onehot", [TILE, SRC_BUFFERS, SRC_PITCH], fp16)
        dst_onehot = sb("dst_onehot", [TILE, TILES_PER_GROUP, WINDOW], fp16)
        src_numbers_i = src_onehot[:, 0:2, :].rearrange("p t n -> p (t n)").bitcast(i32)
        identity_h = sb("identity_h", [WINDOW, WINDOW], fp16)
        counts = sb("counts", [WINDOW, N_NODES], fp16)
        countsT = sb("countsT", [PARTS, BLOCKS, WINDOW], fp16)
        h_parts = [sb(f"h_part{i}", [PARTS, BLOCKS, ROW], bf16) for i in range(3)]
        gate_in = sb("gate_in", [1, 1], i32)
        gate_out = sb("gate_out", [1, 1], i32)

        w_neigh_sb = sb("w_neigh_sb", [ROW, ROW])
        w_self_sb = sb("w_self_sb", [FEAT, FEAT])
        w_edge_sb = sb("w_edge_sb", [EDGE_FEAT + 1, FEAT])
        w1_sb = sb("w1_sb", [FEAT, FEAT])
        w2_sb = sb("w2_sb", [FEAT, FEAT])
        vectors = sb("vectors", [FEAT, 4])
        bn_parts = sb("bn_parts", [FEAT, 2 * N_CHUNKS, 6])
        bn = sb("bn", [FEAT, 2])
        bn_scale = sb("bn_scale", [FEAT, 1])
        bn_shift = sb("bn_shift", [FEAT, 1])
        eps_col = sb("eps_col", [TILE, 1])

        psum = ctx.enter_context(nc.psum_tensor("psum", [TILE, 8, BANK], fp32))
        window_ps = [[psum[:, 0, 0:WINDOW], psum[:, bank, 2 * TILE:2 * TILE + WINDOW]] for bank in (6, 7)]
        starts_ps = psum[:, 0, TILE:TILE + N_GROUPS]
        odd_ps = psum[:, 0, TILE + N_GROUPS:TILE + N_GROUPS + 1]
        half_tiles = TILES_PER_GROUP // 2
        edge_ps = [psum[:, 1 + half, 0:half_tiles * FEAT] for half in range(2)]

        def node_ps(c, width):
            return psum[0:PARTS, 3 + c, 0:CHUNK_BLOCKS * width].rearrange("p (b f) -> p b f", f=width)

        def half_columns(c, half):
            b0, b1_ = HALVES[half]
            return slice(c * CHUNK_NODES + b0 * PARTS, c * CHUNK_NODES + b1_ * PARTS)

        def half_ps(bank, half):
            b0, b1_ = HALVES[half]
            return psum[0:FEAT, bank, 0:(b1_ - b0) * PARTS]

        counts_ps = psum[0:WINDOW, 1:8, :].rearrange("d b n -> d (b n)")
        T_BLOCKS = 2 * BANK // WINDOW
        countsT_chunks = [(b, min(b + T_BLOCKS, BLOCKS)) for b in range(0, BLOCKS, T_BLOCKS)]

        def countsT_ps(n):
            b0, b1_ = countsT_chunks[n]
            bank = psum[0:PARTS, 1 + n, :].bitcast(fp16)
            return bank[:, 0:(b1_ - b0) * WINDOW].rearrange("s (b d) -> s b d", d=WINDOW)

        dense_ps = psum[0:ROW, 7, 2 * TILE:2 * TILE + WINDOW]
        assert len(countsT_chunks) < 7 and N_NODES <= 6 * BANK + 2 * TILE

        T_BANKS = (3, 4, 5, 6)

        x_loaded = [sem(f"x_loaded{c}") for c in range(N_CHUNKS)]
        src_loaded = sem("src_loaded")
        dst_loaded = sem("dst_loaded")
        grp_loaded = sem("grp_loaded")
        weights_loaded = sem("weights_loaded")
        edges_loaded = [sem(f"edges_loaded{k}") for k in range(SLOTS)]
        gathered = [[sem(f"gathered{layer}_{k}") for k in range(SLOTS)] for layer in range(2)]
        numbers_made = sem("numbers_made")
        borders_made = sem("borders_made")
        consts_made = sem("consts_made")
        dve_step = sem("dve_step")
        gate_passed = sem("gate_passed")
        slot_ready = sem("slot_ready")
        var_ready = sem("var_ready")
        std_ready = sem("std_ready")
        std_inv = sem("std_inv")
        h_dve = sem("h_dve")
        h_act = sem("h_act")
        table_written = [sem(f"table_written{layer}") for layer in range(2)]
        transposed = sem("transposed")
        hT_copied = sem("hT_copied")
        self_done = sem("self_done")
        self_added = sem("self_added")
        diag_ready = sem("diag_ready")
        starts_done = sem("starts_done")
        routing_ready = sem("routing_ready")
        onehot_ready = [sem(f"onehot_ready{layer}") for layer in range(2)]
        scattered = [sem(f"scattered{layer}") for layer in range(2)]
        src_numbered = sem("src_numbered")
        src_onehot_ready = sem("src_onehot_ready")
        src_onehot_free = sem("src_onehot_free")
        dst_onehot_ready = sem("dst_onehot_ready")
        counted = sem("counted")
        counts_copied = sem("counts_copied")
        countsT_done = sem("countsT_done")
        countsT_copied = sem("countsT_copied")
        window_added = sem("window_added")
        dense_done = sem("dense_done")
        part_made = sem("part_made")
        rest_made = sem("rest_made")
        pass_shifted = sem("pass_shifted")
        pass_onehot = sem("pass_onehot")
        pass_scattered = sem("pass_scattered")
        sums_cleared = sem("sums_cleared")
        sums_done = sem("sums_done")
        neigh_done = sem("neigh_done")
        node_sums_read = sem("node_sums_read")
        edge_terms = sem("edge_terms")
        summed = sem("summed")
        message_ready = sem("message_ready")
        hT_summed = sem("hT_summed")
        mm1_done = sem("mm1_done")
        r1_ready = sem("r1_ready")
        mm2_done = sem("mm2_done")
        h2_ready = sem("h2_ready")
        bn_var = sem("bn_var")
        bn_std = sem("bn_std")
        bn_ready = sem("bn_ready")
        resultT_ready = sem("resultT_ready")
        result_done = sem("result_done")
        out_ready = sem("out_ready")
        out_written = sem("out_written")

        b1_col, b2_col, gamma_col, beta_col = (vectors[:, i:i + 1] for i in range(4))
        N_WEIGHTS = 10

        block = ctx.enter_context(nc.Block())

        @block.sync
        def _(sp):
            for c in range(N_CHUNKS):
                for p0, p1 in PART_SPANS:
                    sp.dma_start(x_sb[p0:p1, chunk_blocks(c)],
                                 node_major(x)[p0:p1, chunk_blocks(c)]).then_inc(x_loaded[c], 16)
            for layer in range(2):
                for c in range(N_CHUNKS):
                    sp.wait_ge(h_dve, layer * N_CHUNKS + c + 1)
                    sp.wait_ge(h_act, layer * N_CHUNKS + c + 1)
                    for p0, p1 in PART_SPANS:
                        sp.dma_start(node_major(tables[layer])[p0:p1, chunk_blocks(c)],
                                     h[p0:p1, chunk_blocks(c)]).then_inc(table_written[layer], 16)
                if layer == 0:
                    for k in range(SLOTS):
                        sp.dma_start(edges[0:EDGE_FEAT, k, :], edge_attr[k]).then_inc(edges_loaded[k], 16)
            with sp.Fori(1, ROUNDS) as r:
                for k in range(SLOTS):
                    sp.wait_ge(edge_terms, (r - 1) * SLOTS + k + 1)
                    sp.dma_start(edges[0:EDGE_FEAT, k, :],
                                 edge_attr[bass.ds(r * SLOTS + k, 1)].rearrange("g f e -> (g f) e")
                                 ).then_inc(edges_loaded[k], 16)
            for c in range(N_CHUNKS):
                sp.wait_ge(out_ready, c + 1)
                for p0, p1 in PART_SPANS:
                    sp.dma_start(node_major(out)[p0:p1, chunk_blocks(c)],
                                 x_mid[p0:p1, chunk_blocks(c)]).then_inc(out_written, 16)
            for written in (*table_written, out_written):
                sp.wait_ge(written, 32 * N_CHUNKS)

        @block.gpsimd
        def _(pool):
            nc.gpsimd.iota(columns_i[:], pattern=[[1, TILE]], base=0, channel_multiplier=0)
            nc.gpsimd.iota(windows_i[:], pattern=[[WINDOW, N_WINDOWS]], base=0, channel_multiplier=0)
            nc.gpsimd.iota(part_i[:], pattern=[[0, 1]], base=0, channel_multiplier=1)
            nc.gpsimd.drain().then_inc(numbers_made, 1)
            nc.gpsimd.memset(gate_in[:], 0).then_inc(gate_passed, 1)
            nc.gpsimd.iota(src_numbers_i, pattern=[[1, SRC_PITCH]], base=-SRC_SHIFT, channel_multiplier=0)
            nc.gpsimd.drain().then_inc(numbers_made, 1)
            pool.wait_ge(numbers_made, 2)
            nc.gpsimd.tensor_copy(src_numbers[:], src_numbers_i).then_inc(src_numbered, 1)
            pool.wait_ge(src_numbered, 1)
            nc.gpsimd.memset(edges[EDGE_FEAT:, :, :], 1.0).then_inc(sums_cleared, 1)
            for layer in range(2):
                pool.wait_ge(sums_cleared, layer + 1)
                nc.gpsimd.memset(sums[layer][:], 0.0).then_inc(sums_cleared, 1)

            def gather_group(layer, r, k):
                if k % 2 == 0:
                    pool.wait_ge(gate_passed, (layer * N_GROUPS + r * SLOTS + k) // 2 + 1)
                    pool.wait_ge(slot_ready, layer * N_GROUPS + r * SLOTS + k + 2)
                    nc.gpsimd.tensor_tensor(gate_out[:], gate_in[:], gate_in[:],
                                            ALU.add).then_inc(gate_passed, 1)
                for j in range(TILES_PER_GROUP):
                    nc.gpsimd.indirect_dma_start(
                        out=rows[:, k, j, 0:FEAT], out_offset=None, in_=tables[layer],
                        in_offset=bass.IndirectOffsetOnAxis(ap=slot_idx[:, k, j:j + 1], axis=0),
                    ).then_inc(gathered[layer][k], 16)

            pool.wait_ge(table_written[0], 32 * N_CHUNKS)
            for k in range(DENSE_K):
                gather_group(0, 0, k)
            pool.wait_ge(routing_ready, 1)
            odd = pool.value_load(odd_i[0:1, 0:1], min_val=0, max_val=2 * N_GROUPS)
            with pool.If(odd):
                gather_group(0, 0, DENSE_K)
                with pool.Fori(1, ROUNDS) as r:
                    for k in range(SLOTS):
                        gather_group(0, r, k)
            with pool.Else():
                with pool.Fori(1, ROUNDS) as r:
                    for k in range(DENSE_K):
                        gather_group(0, r, k)
            pool.wait_ge(table_written[1], 32 * N_CHUNKS)
            with pool.Fori(0, ROUNDS) as r:
                for k in range(SLOTS):
                    gather_group(1, r, k)

        @block.vector
        def _(dve):
            steps = [0]

            def chained(instruction):
                steps[0] += 1
                instruction.then_inc(dve_step, 1)
                dve.wait_ge(dve_step, steps[0])

            def statistics(features, c):
                blocks = range(c * CHUNK_BLOCKS, (c + 1) * CHUNK_BLOCKS)
                for b in blocks:
                    last = nc.vector.bn_stats(block_stats[:, b], features[:, b])
                chained(last)
                for b in blocks:
                    last = nc.vector.bn_aggr(mean_var[:, b], block_stats[:, b])
                last.then_inc(var_ready, 1)

            def normalise(features, c, layer):
                here = chunk_blocks(c)
                dve.wait_ge(std_ready, layer * N_CHUNKS + c + 1)
                chained(nc.vector.reciprocal(rstd[:, here], rstd[:, here]))
                nc.vector.scalar_tensor_tensor(neg_mean_rstd[:, here], mean_var[:, here, 0], -1.0, rstd[:, here],
                                               ALU.mult, ALU.mult).then_inc(std_inv, 1)
                own = range(c * CHUNK_BLOCKS, c * CHUNK_BLOCKS + DVE_BLOCKS)
                for b in own:
                    last = nc.vector.tensor_scalar(h[:, b], features[:, b], mean_var[:, b, 0:1], 0.0,
                                                   ALU.subtract, ALU.max)
                chained(last)
                for b in own:
                    last = nc.vector.tensor_scalar(h[:, b], h[:, b], rstd[:, b:b + 1], None, ALU.mult)
                last.then_inc(h_dve, 1)

            nc.vector.memset(eps_col[:], EPS).then_inc(consts_made, 1)
            for c in range(N_CHUNKS):
                dve.wait_ge(x_loaded[c], 32)
                statistics(x_sb, c)
                if c > 0:
                    normalise(x_sb, c - 1, 0)
            normalise(x_sb, N_CHUNKS - 1, 0)

            dve.wait_ge(src_loaded, 32)
            nc.vector.tensor_copy(slot_idx[:].rearrange("p s t -> p (s t)"),
                                  src_idx[:, 0:SLOTS * TILES_PER_GROUP]).then_inc(slot_ready, SLOTS)

            nc.vector.tensor_scalar(src_f[:], src_idx[:, 0:N_TILES], float(SRC_SHIFT), None, ALU.subtract)
            chained(nc.vector.memset(ones[:], 1.0))
            dve.wait_ge(src_numbered, 1)

            def source_onehot(tile, n):
                return nc.vector.tensor_scalar(src_onehot[:, n % SRC_BUFFERS], src_numbers[:], src_f[:, tile], None,
                                               ALU.is_equal).then_inc(src_onehot_ready, 1)

            for j in range(SRC_BUFFERS):
                tile = DENSE_K * TILES_PER_GROUP + j
                source_onehot(slice(tile, tile + 1), j)

            chained(nc.vector.memset(w_neigh_sb[:], 0.0))
            nc.vector.drain().then_inc(src_onehot_free, SRC_BUFFERS)
            nc.vector.memset(w_neigh_sb[FEAT:ROW, FEAT:ROW], 1.0).then_inc(borders_made, 1)
            nc.vector.memset(rows[:, :, :, FEAT:ROW], 1.0)
            for i, part in enumerate(h_parts):
                nc.vector.memset(part[:, :, FEAT:ROW], 1.0 if i == 0 else 0.0)
            dve.wait_ge(numbers_made, 1)
            nc.vector.tensor_copy(windows_f[:], windows_i[:])
            nc.vector.tensor_copy(columns_f[:], columns_i[:])
            chained(nc.vector.tensor_copy(part_f[:], part_i[:]))
            nc.vector.tensor_scalar(identity[:], columns_f[:], part_f[:], None, ALU.is_equal)
            nc.vector.tensor_scalar(identity_h[:], columns_f[0:WINDOW, 0:WINDOW], part_f[0:WINDOW], None,
                                    ALU.is_equal)
            nc.vector.drain().then_inc(consts_made, 1)

            dve.wait_ge(grp_loaded, 16)
            nc.vector.tensor_reduce(grp_min[:], grp_i[:], AX, ALU.min)
            nc.vector.tensor_reduce(grp_max[:], grp_i[:], AX, ALU.max)
            chained(nc.vector.memset(grp_odd[:], 0.0))
            for c in range(N_CHUNKS - 1):
                nc.vector.tensor_scalar(grp_odd[:, 1:2], part_f[0:N_GROUPS], float(CHUNK_ROUNDS[c][1] * SLOTS),
                                        float(CHUNK_NODES), ALU.is_ge, ALU.mult)
                chained(nc.vector.drain())
                chained(nc.vector.tensor_tensor(grp_odd[:, 0:1], grp_odd[:, 0:1], grp_odd[:, 1:2], ALU.add))
            chained(nc.vector.tensor_tensor(grp_odd[:, 2:3], grp_min[:], grp_odd[:, 0:1], ALU.is_lt))
            chained(nc.vector.tensor_tensor(grp_odd[:, 3:4], grp_max[:], grp_min[:], ALU.subtract))
            chained(nc.vector.tensor_scalar(grp_odd[:, 3:4], grp_odd[:, 3:4], float(WINDOW), None, ALU.is_ge))
            chained(nc.vector.tensor_tensor(grp_odd[:, 3:4], grp_odd[:, 3:4], grp_odd[:, 2:3], ALU.add))
            nc.vector.tensor_scalar(grp_diag[:], identity[0:N_GROUPS, 0:N_GROUPS], grp_min[:], None,
                                    ALU.mult).then_inc(diag_ready, 1)

            dve.wait_ge(dst_loaded, 16)
            chained(nc.vector.tensor_copy(dst_f[:], dst_i[:]))
            chained(nc.vector.memset(dst_f[:, LAST_TILE:], -1e6))
            chained(nc.vector.tensor_copy(dst_f[0:LAST_ROWS, LAST_TILE:], dst_i[0:LAST_ROWS, LAST_TILE:]))
            dve.wait_ge(starts_done, 1)
            nc.vector.tensor_tensor(
                dst_rel[:].rearrange("p (g t) -> p g t", t=TILES_PER_GROUP),
                dst_f[:].rearrange("p (g t) -> p g t", t=TILES_PER_GROUP),
                starts_ps.rearrange("p (g o) -> p g o", o=1).to_broadcast(
                    [TILE, N_GROUPS, TILES_PER_GROUP]), ALU.subtract)
            nc.vector.tensor_copy(starts_i[:], starts_ps[0:1])
            chained(nc.vector.tensor_copy(odd_i[:], odd_ps[0:1]))
            nc.vector.drain().then_inc(routing_ready, 1)

            def make_onehot(dst_of_edge, made):
                shape = [TILE, TILES_PER_GROUP, WINDOW]
                return nc.vector.tensor_tensor(
                    made[:], columns_f[:, 0:WINDOW].rearrange("p (o n) -> p o n", o=1).to_broadcast(shape),
                    dst_of_edge.rearrange("p (t o) -> p t o", o=1).to_broadcast(shape), ALU.is_equal)

            make_onehot(dst_rel[:, DENSE_K * TILES_PER_GROUP:SLOTS * TILES_PER_GROUP],
                        dst_onehot).then_inc(dst_onehot_ready, 1)

            def add_self_terms():
                for c in range(N_CHUNKS):
                    dve.wait_ge(self_done, c + 1)
                    nc.vector.tensor_tensor(x_mid[:, chunk_blocks(c)], x_sb[:, chunk_blocks(c)], node_ps(c, FEAT),
                                            ALU.add).then_inc(self_added, 1)

            def add_edge_terms(group, k, r):
                dve.wait_ge(gathered[1][k], (r + 1) * 16 * TILES_PER_GROUP)
                dve.wait_ge(edge_terms, group + 1)
                for half in range(2):
                    tiles = slice(half * half_tiles, (half + 1) * half_tiles)
                    nc.vector.tensor_tensor(
                        message[:, tiles], rows[:, k, tiles, 0:FEAT],
                        edge_ps[half].rearrange("p (t f) -> p t f", f=FEAT), ALU.add).then_inc(summed, 1)

            def add_window(layer, start, made):
                window = sums[layer][:, bass.ds(start, WINDOW)]
                return nc.vector.tensor_tensor(window, window, made[0:ROW], ALU.add)

            def dense_onehots(r, tiles):
                group = r * SLOTS + DENSE_K
                if 0 in tiles:
                    make_onehot(dst_rel[:, bass.ds(group * TILES_PER_GROUP, TILES_PER_GROUP)],
                                dst_onehot).then_inc(dst_onehot_ready, 1)
                for j in tiles:
                    dve.wait_ge(src_onehot_free, r * TILES_PER_GROUP + j + 1)
                    source_onehot(bass.ds(group * TILES_PER_GROUP + j, 1), j)

            def split_features():
                for i in range(2):
                    dve.wait_ge(part_made, i + 1)
                    nc.vector.tensor_tensor(h_rest[:], (h, h_rest)[i][:], h_parts[i][:, :, 0:FEAT],
                                            ALU.subtract).then_inc(rest_made, 1)

            def dense_round(r, first=False, last=False):
                dense_onehots(r, range(SRC_BUFFERS, TILES_PER_GROUP))
                group_onehot(0, r, 0)
                group_onehot(0, r, 1)
                if first:
                    split_features()
                scatter_group(0, r, 0, general=False, order=None if first else r * SLOTS)
                group_onehot(0, r, 2)
                scatter_group(0, r, 1, general=False, order=r * SLOTS + 1)
                start = group_start(r * SLOTS + DENSE_K)
                dve.wait_ge(dense_done, r + 1)
                dve.wait_ge(window_added, r * SLOTS + 2)
                add_window(0, start, dense_ps).then_inc(window_added, 1)
                nc.vector.drain().then_inc(slot_ready, 1)
                if not last:
                    dense_onehots(r + 1, range(SRC_BUFFERS))
                scatter_group(0, r, 2, general=False, order=r * SLOTS + 3)

            def refill_slot(group, k):
                nc.vector.tensor_copy(
                    slot_idx[:, k, :],
                    src_idx[:, bass.ds((group + SLOTS) * TILES_PER_GROUP, TILES_PER_GROUP)]
                ).then_inc(slot_ready, 1)

            def group_onehot(layer, r, k):
                group_tiles = bass.ds((r * SLOTS + k) * TILES_PER_GROUP, TILES_PER_GROUP)
                make_onehot(dst_rel[:, group_tiles], onehot[k % 2]).then_inc(onehot_ready[layer], 1)

            def group_start(group):
                return dve.value_load(starts_i[0:1, bass.ds(group, 1)], min_val=0, max_val=N_NODES - 1)

            def scatter_group(layer, r, k, general, order=None):
                group = r * SLOTS + k
                group_tiles = bass.ds(group * TILES_PER_GROUP, TILES_PER_GROUP)
                if not general:
                    start = group_start(group)
                    if layer == 1:
                        group_onehot(layer, r, k)
                if layer == 1:
                    add_edge_terms(group, k, r)
                    if not general:
                        refill_slot(group, k)
                if not general:
                    dve.wait_ge(scattered[layer], (r * DENSE_K + k if layer == 0 else group) + 1)
                    if order is not None:
                        dve.wait_ge(window_added, order)
                    added = add_window(layer, start, window_ps[layer][k % 2])
                    if layer == 0:
                        added.then_inc(window_added, 1)
                else:
                    with dve.Fori(0, N_WINDOWS) as w:
                        passes = (layer * N_GROUPS + group) * N_WINDOWS + w
                        nc.vector.tensor_tensor(
                            dst_pass[:], dst_f[:, group_tiles],
                            windows_f[:, bass.ds(w, 1)].to_broadcast([TILE, TILES_PER_GROUP]),
                            ALU.subtract).then_inc(pass_shifted, 1)
                        dve.wait_ge(pass_shifted, passes + 1)
                        make_onehot(dst_pass[:], onehot[0]).then_inc(pass_onehot, 1)
                        dve.wait_ge(pass_scattered, passes + 1)
                        add_window(layer, w * WINDOW, window_ps[layer][0])
                if layer == 0 or general:
                    refill_slot(group, k)

            def finish_chunk(layer, c, general):
                chained(nc.vector.drain())
                if layer == 0:
                    sums_ready_c = nc.vector.drain()
                    sums_ready_c.then_inc(sums_done, 1)
                    here = chunk_blocks(c)
                    dve.wait_ge(neigh_done, c + 1)
                    chained(nc.vector.tensor_scalar(degree[:, here], node_ps(c, ROW)[:, :, FEAT], 1.0, None, ALU.max))
                    chained(nc.vector.reciprocal(degree[:, here], degree[:, here]))
                    for b in range(CHUNK_BLOCKS):
                        node_b = c * CHUNK_BLOCKS + b
                        last = nc.vector.scalar_tensor_tensor(
                            x_mid[:, node_b], node_ps(c, ROW)[:, b, 0:FEAT], degree[:, node_b:node_b + 1],
                            x_mid[:, node_b], ALU.mult, ALU.add)
                    chained(last)
                    nc.vector.drain().then_inc(node_sums_read, 1)
                    statistics(x_mid, c)
                    if c == 0:
                        dve.wait_ge(table_written[0], 32 * N_CHUNKS)
                        dve.wait_ge(transposed, 2 * N_CHUNKS)
                        if not general:
                            dve.wait_ge(part_made, 3)
                    normalise(x_mid, c, 1)
                else:
                    dve.wait_ge(hT_copied, 4 * N_CHUNKS)
                    here = slice(c * CHUNK_NODES, (c + 1) * CHUNK_NODES)
                    nc.vector.tensor_tensor(hT[:, here], hT[:, here], sums[1][0:FEAT, here],
                                            ALU.add).then_inc(hT_summed, 1)
                    for half in range(2):
                        dve.wait_ge(mm2_done, 2 * c + half + 1)
                        cols = h2T[:, half_columns(c, half)]
                        chained(nc.vector.tensor_scalar(cols, half_ps(5 + half, half), b2_col, None, ALU.add))
                        nc.vector.bn_stats(bn_parts[:, 2 * c + half, :], cols).then_inc(h2_ready, 1)

            odd = dve.value_load(odd_i[0:1, 0:1], min_val=0, max_val=2 * N_GROUPS)
            dve.wait_ge(weights_loaded, 16 * N_WEIGHTS)
            dve.wait_ge(sums_cleared, 3)

            def run_layer(layer, general):
                if general:
                    if layer == 0:
                        add_self_terms()
                    with dve.Fori(0, ROUNDS) as r:
                        for k in range(SLOTS):
                            scatter_group(layer, r, k, general=True)
                    for c in range(N_CHUNKS):
                        finish_chunk(layer, c, general)
                else:
                    for c, (r0, r1) in enumerate(CHUNK_ROUNDS):
                        if layer == 0 and c == 0:
                            dense_round(0, first=True)
                            add_self_terms()
                            r0 = 1
                        if layer == 0 and c == N_CHUNKS - 1:
                            assert r1 == r0 + 1
                            dense_round(r0, last=True)
                        elif layer == 0:
                            with dve.Fori(r0, r1) as r:
                                dense_round(r)
                        else:
                            with dve.Fori(r0, r1) as r:
                                for k in range(SLOTS):
                                    scatter_group(layer, r, k, general=False)
                        finish_chunk(layer, c, general)

            for layer in range(2):
                before = steps[0]
                with dve.If(odd):
                    run_layer(layer, general=True)
                after = steps[0]
                steps[0] = before
                with dve.Else():
                    run_layer(layer, general=False)
                assert steps[0] == after

            dve.wait_ge(h2_ready, 2 * N_CHUNKS)
            nc.vector.bn_aggr(bn[:], bn_parts[:].rearrange("f c s -> f (c s)")).then_inc(bn_var, 1)
            dve.wait_ge(bn_std, 1)
            chained(nc.vector.reciprocal(bn_scale[:], bn_scale[:]))
            chained(nc.vector.tensor_tensor(bn_scale[:], bn_scale[:], gamma_col, ALU.mult))
            chained(nc.vector.tensor_tensor(bn_shift[:], bn[:, 0:1], bn_scale[:], ALU.mult))
            nc.vector.tensor_tensor(bn_shift[:], beta_col, bn_shift[:], ALU.subtract).then_inc(bn_ready, 1)
            for c in range(N_CHUNKS):
                dve.wait_ge(result_done, c + 1)
                nc.vector.tensor_tensor(x_mid[:, chunk_blocks(c)], x_mid[:, chunk_blocks(c)],
                                        node_ps(c, FEAT), ALU.add).then_inc(out_ready, 1)

        @block.scalar
        def _(act):
            act.dma_start(src_idx[:, 0:N_TILES], src).then_inc(src_loaded, 16)
            act.dma_start(src_idx[:, N_TILES:], src[:, 0:SLOTS * TILES_PER_GROUP]).then_inc(src_loaded, 16)
            act.dma_start(grp_i[:], dst_grouped).then_inc(grp_loaded, 16)
            act.dma_start(dst_i[:], dst).then_inc(dst_loaded, 16)

            def deviations(layer, c):
                act.wait_ge(var_ready, layer * N_CHUNKS + c + 1)
                nc.scalar.activation(rstd[:, chunk_blocks(c)], mean_var[:, chunk_blocks(c), 1], ACT.Sqrt,
                                     bias=eps_col[0:PARTS]).then_inc(std_ready, 1)

            def normalise(features, layer, c):
                act.wait_ge(std_inv, layer * N_CHUNKS + c + 1)
                for b in range(c * CHUNK_BLOCKS + DVE_BLOCKS, (c + 1) * CHUNK_BLOCKS):
                    last = nc.scalar.activation(h[:, b], features[:, b], ACT.Relu, bias=neg_mean_rstd[:, b:b + 1],
                                                scale=rstd[:, b:b + 1])
                last.then_inc(h_act, 1)

            def copy_transposed(layer):
                for n in range(2 * N_CHUNKS):
                    c, half = divmod(n, 2)
                    act.wait_ge(transposed, layer * 2 * N_CHUNKS + n + 1)
                    nc.scalar.copy(hT[:, half_columns(c, half)],
                                   half_ps(T_BANKS[n % 4], half)).then_inc(hT_copied, 1)

            act.wait_ge(consts_made, 1)
            for c in range(N_CHUNKS):
                deviations(0, c)
                normalise(x_sb, 0, c)
            for dst_ap, src_ap in ((w_self_sb[:], w_self), (w_edge_sb[0:EDGE_FEAT], w_edge),
                                   (w_edge_sb[EDGE_FEAT:], b_edge), (w1_sb[:], w1), (w2_sb[:], w2),
                                   (b1_col, b1), (b2_col, b2), (gamma_col, gamma), (beta_col, beta)):
                act.dma_start(dst_ap, src_ap).then_inc(weights_loaded, 16)
            act.wait_ge(borders_made, 1)
            act.dma_start(w_neigh_sb[0:FEAT, 0:FEAT], w_neigh).then_inc(weights_loaded, 16)
            def round_part(i):
                if i > 0:
                    act.wait_ge(rest_made, i)
                nc.scalar.copy(h_parts[i][:, :, 0:FEAT], (h if i == 0 else h_rest)[:]).then_inc(part_made, 1)

            def copy_counts(r):
                act.wait_ge(counted, r + 1)
                nc.scalar.copy(counts[:], counts_ps[:, 0:N_NODES]).then_inc(counts_copied, 1)
                act.wait_ge(countsT_done, r + 1)
                for n, (b0, b1_) in enumerate(countsT_chunks):
                    last = nc.scalar.copy(countsT[:, b0:b1_], countsT_ps(n))
                last.then_inc(countsT_copied, 1)

            def finish_features(c):
                deviations(1, c)
                normalise(x_mid, 1, c)

            act.wait_ge(routing_ready, 1)
            odd = act.value_load(odd_i[0:1, 0:1], min_val=0, max_val=2 * N_GROUPS)
            with act.If(odd):
                copy_transposed(0)
                for c in range(N_CHUNKS):
                    finish_features(c)
            with act.Else():
                act.wait_ge(h_dve, N_CHUNKS)
                act.wait_ge(h_act, N_CHUNKS)
                for i in range(3):
                    round_part(i)
                for c, (r0, r1) in enumerate(CHUNK_ROUNDS):
                    if c == 0:
                        copy_counts(0)
                        copy_transposed(0)
                        r0 = 1
                    with act.Fori(r0, r1) as r:
                        copy_counts(r)
                    finish_features(c)
            act.wait_ge(self_done, N_CHUNKS)
            copy_transposed(1)

            def relu_messages(group):
                for half in range(2):
                    tiles = slice(half * half_tiles, (half + 1) * half_tiles)
                    act.wait_ge(summed, 2 * group + half + 1)
                    nc.scalar.activation(message[:, tiles], message[:, tiles], ACT.Relu).then_inc(message_ready, 1)

            def hidden_layer(c):
                for half in range(2):
                    act.wait_ge(mm1_done, 2 * c + half + 1)
                    nc.scalar.activation(r1T[:, half_columns(c, half)], half_ps(3 + half, half), ACT.Relu,
                                         bias=b1_col).then_inc(r1_ready, 1)

            act.wait_ge(weights_loaded, 16 * N_WEIGHTS)
            with act.If(odd):
                with act.Fori(0, N_GROUPS) as group:
                    relu_messages(group)
                for c in range(N_CHUNKS):
                    hidden_layer(c)
            with act.Else():
                for c, (r0, r1) in enumerate(CHUNK_ROUNDS):
                    with act.Fori(r0 * SLOTS, r1 * SLOTS) as group:
                        relu_messages(group)
                    hidden_layer(c)
            act.wait_ge(bn_var, 1)
            nc.scalar.activation(bn_scale[:], bn[:, 1:2], ACT.Sqrt, bias=eps_col[0:FEAT]).then_inc(bn_std, 1)
            act.wait_ge(bn_ready, 1)
            act.wait_ge(mm2_done, 2 * N_CHUNKS)
            for c in range(N_CHUNKS):
                here = slice(c * CHUNK_NODES, (c + 1) * CHUNK_NODES)
                nc.scalar.activation(r1T[:, here], h2T[:, here], ACT.Relu, bias=bn_shift[:],
                                     scale=bn_scale[:]).then_inc(resultT_ready, 1)

        @block.tensor
        def _(pe):
            def transpose_h(layer):
                for n in range(2 * N_CHUNKS):
                    c, half = divmod(n, 2)
                    b0, b1_ = HALVES[half]
                    pe.wait_ge(h_dve, layer * N_CHUNKS + c + 1)
                    pe.wait_ge(h_act, layer * N_CHUNKS + c + 1)
                    if n >= 4:
                        pe.wait_ge(hT_copied, layer * 2 * N_CHUNKS + n - 3)
                    for b in range(b0, b1_):
                        last = nc.tensor.transpose(
                            half_ps(T_BANKS[n % 4], half)[:, (b - b0) * PARTS:(b - b0 + 1) * PARTS],
                            h[:, c * CHUNK_BLOCKS + b, :], identity[0:PARTS, 0:PARTS])
                    last.then_inc(transposed, 1)

            pe.wait_ge(consts_made, 2)
            pe.wait_ge(diag_ready, 1)
            nc.tensor.matmul(starts_ps, ones[:], grp_diag[:], start=True, stop=True)
            nc.tensor.matmul(odd_ps, ones[:], grp_odd[:, 3:4], start=True, stop=True).then_inc(starts_done, 1)

            def self_terms():
                transpose_h(0)
                pe.wait_ge(weights_loaded, 16 * N_WEIGHTS)
                pe.wait_ge(hT_copied, 2 * N_CHUNKS)
                for c in range(N_CHUNKS):
                    for b in range(CHUNK_BLOCKS):
                        first = (c * CHUNK_BLOCKS + b) * PARTS
                        last = nc.tensor.matmul(node_ps(c, FEAT)[:, b, :], hT[:, first:first + PARTS],
                                                w_self_sb[:], start=True, stop=True)
                    last.then_inc(self_done, 1)
                pe.wait_ge(self_added, N_CHUNKS)

            def scatter(layer, width, lhs, place, counter, halfway=None):
                for j in range(TILES_PER_GROUP):
                    if halfway and j == half_tiles:
                        pe.wait_ge(*halfway)
                    last = nc.tensor.matmul(window_ps[layer][place][0:width], lhs(j), onehot[place][:, j, :],
                                            start=(j == 0), stop=(j == TILES_PER_GROUP - 1))
                last.then_inc(counter, 1)

            def scatter_group(layer, r, k, general):
                group = r * SLOTS + k
                if layer == 0:
                    lhs, lhs_there = (lambda j: rows[:, k, j, :]), (gathered[0][k], (r + 1) * 16 * TILES_PER_GROUP)
                    halfway = None
                else:
                    pe.wait_ge(edges_loaded[k], (r + 1) * 16)
                    for j in range(TILES_PER_GROUP):
                        half, place = divmod(j, half_tiles)
                        last = nc.tensor.matmul(edge_ps[half][:, place * FEAT:(place + 1) * FEAT],
                                                edges[:, k, j * TILE:(j + 1) * TILE], w_edge_sb[:],
                                                start=True, stop=True)
                    last.then_inc(edge_terms, 1)
                    lhs, lhs_there = (lambda j: message[:, j, :]), (message_ready, 2 * group + 1)
                    halfway = (message_ready, 2 * group + 2)
                width = ROW if layer == 0 else FEAT
                if not general:
                    pe.wait_ge(*lhs_there)
                    pe.wait_ge(onehot_ready[layer], (r * DENSE_K + k if layer == 0 else group) + 1)
                    scatter(layer, width, lhs, k % 2, scattered[layer], halfway)
                else:
                    with pe.Fori(0, N_WINDOWS) as w:
                        pe.wait_ge(*lhs_there)
                        pe.wait_ge(pass_onehot, (layer * N_GROUPS + group) * N_WINDOWS + w + 1)
                        scatter(layer, width, lhs, 0, pass_scattered, halfway)

            def finish_chunk(layer, c):
                if layer == 0:
                    pe.wait_ge(sums_done, c + 1)
                    for b in range(CHUNK_BLOCKS):
                        first = (c * CHUNK_BLOCKS + b) * PARTS
                        last = nc.tensor.matmul(node_ps(c, ROW)[:, b, :], sums[0][:, first:first + PARTS],
                                                w_neigh_sb[:], start=True, stop=True)
                    last.then_inc(neigh_done, 1)
                    pe.wait_ge(node_sums_read, c + 1)
                    nc.tensor.drain()
                else:
                    pe.wait_ge(hT_summed, c + 1)
                    for half in range(2):
                        nc.tensor.matmul(half_ps(3 + half, half), w1_sb[:], hT[:, half_columns(c, half)],
                                         start=True, stop=True).then_inc(mm1_done, 1)
                    for half in range(2):
                        pe.wait_ge(r1_ready, 2 * c + half + 1)
                        if c > 0:
                            pe.wait_ge(h2_ready, 2 * c)
                        nc.tensor.matmul(half_ps(5 + half, half), w2_sb[:], r1T[:, half_columns(c, half)],
                                         start=True, stop=True).then_inc(mm2_done, 1)

            def count_edges(r):
                pe.wait_ge(dst_onehot_ready, r + 1)
                for j in range(TILES_PER_GROUP):
                    pe.wait_ge(src_onehot_ready, r * TILES_PER_GROUP + j + 1)
                    for first in range(0, N_NODES, BANK):
                        here = slice(first, min(first + BANK, N_NODES))
                        last = nc.tensor.matmul(counts_ps[:, here], dst_onehot[:, j, :],
                                                src_onehot[:, j % SRC_BUFFERS, here],
                                                start=(j == 0), stop=(j == TILES_PER_GROUP - 1))
                    last.then_inc(src_onehot_free, 1)
                nc.tensor.drain().then_inc(counted, 1)

            def transpose_counts(r):
                pe.wait_ge(counts_copied, r + 1)
                for n, (b0, b1_) in enumerate(countsT_chunks):
                    for b in range(b0, b1_):
                        last = nc.tensor.transpose(countsT_ps(n)[:, b - b0, :],
                                                   counts[:, b * PARTS:(b + 1) * PARTS], identity_h[:])
                last.then_inc(countsT_done, 1)

            def multiply_counts(r):
                pe.wait_ge(part_made, 3)
                pe.wait_ge(countsT_copied, r + 1)
                for b in range(BLOCKS):
                    for i, part in enumerate(h_parts):
                        last = nc.tensor.matmul(dense_ps, part[:, b, :], countsT[:, b, :],
                                                start=(b == 0 and i == 0), stop=(b == BLOCKS - 1 and i == 2))
                last.then_inc(dense_done, 1)

            def dense_round(r):
                count_edges(r)
                scatter_group(0, r, 0, general=False)
                transpose_counts(r)
                scatter_group(0, r, 1, general=False)
                multiply_counts(r)
                scatter_group(0, r, 2, general=False)

            pe.wait_ge(routing_ready, 1)
            odd = pe.value_load(odd_i[0:1, 0:1], min_val=0, max_val=2 * N_GROUPS)
            for layer in range(2):
                if layer == 1:
                    transpose_h(1)
                    pe.wait_ge(hT_copied, 4 * N_CHUNKS)
                with pe.If(odd):
                    if layer == 0:
                        self_terms()
                    with pe.Fori(0, ROUNDS) as r:
                        for k in range(SLOTS):
                            scatter_group(layer, r, k, general=True)
                    for c in range(N_CHUNKS):
                        finish_chunk(layer, c)
                with pe.Else():
                    for c, (r0, r1) in enumerate(CHUNK_ROUNDS):
                        if layer == 0 and c == 0:
                            dense_round(0)
                            pe.wait_ge(window_added, SLOTS - 1)
                            self_terms()
                            r0 = 1
                        with pe.Fori(r0, r1) as r:
                            if layer == 0:
                                dense_round(r)
                            else:
                                for k in range(SLOTS):
                                    scatter_group(layer, r, k, general=False)
                        finish_chunk(layer, c)

            for c in range(N_CHUNKS):
                pe.wait_ge(resultT_ready, c + 1)
                for b in range(CHUNK_BLOCKS):
                    first = (c * CHUNK_BLOCKS + b) * PARTS
                    last = nc.tensor.transpose(node_ps(c, FEAT)[:, b, :], r1T[:, first:first + PARTS],
                                               identity[0:FEAT, 0:FEAT])
                last.then_inc(result_done, 1)


def kernel(x, src, dst, edge_attr_32, L0_gnn_W, L0_gnn_B, L1_gnn_We, L1_gnn_be, L1_gnn_W1, L1_gnn_b1,
           L1_gnn_W2, L1_gnn_b2, L1_gnn_gamma, L1_gnn_beta):
    import numpy as np
    import concourse.bacc as bacc
    from concourse.bass_utils import run_bass_kernel_spmd

    pad = PADDED_EDGES - N_EDGES
    src_p = np.pad(np.asarray(src), (0, pad))
    dst_p = np.pad(np.asarray(dst), (0, pad), mode="edge")
    edge_p = np.pad(np.asarray(edge_attr_32), ((0, pad), (0, 0)))
    arrays = {
        "x": np.asarray(x),
        "src": src_p.reshape(N_TILES, TILE).T,
        "dst": dst_p.reshape(N_TILES, TILE).T,
        "dst_grouped": dst_p.reshape(N_GROUPS, GROUP),
        "edge_attr": edge_p.reshape(N_GROUPS, GROUP, EDGE_FEAT).transpose(0, 2, 1),
        "w_neigh": np.asarray(L0_gnn_W).T,
        "w_self": np.asarray(L0_gnn_B).T,
        "w_edge": np.asarray(L1_gnn_We),
        "b_edge": np.asarray(L1_gnn_be).reshape(1, FEAT),
        "w1": np.asarray(L1_gnn_W1),
        "b1": np.asarray(L1_gnn_b1).reshape(FEAT, 1),
        "w2": np.asarray(L1_gnn_W2),
        "b2": np.asarray(L1_gnn_b2).reshape(FEAT, 1),
        "gamma": np.asarray(L1_gnn_gamma).reshape(FEAT, 1),
        "beta": np.asarray(L1_gnn_beta).reshape(FEAT, 1),
    }
    arrays = {name: np.ascontiguousarray(a) for name, a in arrays.items()}
    nc = bacc.Bacc("TRN2", target_bir_lowering=False, num_devices=1)
    args = [nc.dram_tensor(name, a.shape, mybir.dt.from_np(a.dtype), kind="ExternalInput").ap()
            for name, a in arrays.items()]
    out = nc.dram_tensor("out", (N_NODES, FEAT), mybir.dt.float32, kind="ExternalOutput").ap()
    gnn_two_layers(nc, *args, out)
    result = run_bass_kernel_spmd(nc, [arrays], core_ids=[0])
    return result.results[0]["out"]
```

```python
import concourse.bass as bass
from concourse import mybir
from contextlib import ExitStack

N_NODES = 3125
FEAT = 96
EDGE_FEAT = 32
N_EDGES = 53125

TILE = 128
TILES_PER_GROUP = 8
GROUP = TILE * TILES_PER_GROUP
N_GROUPS = -(-N_EDGES // GROUP)
N_TILES = N_GROUPS * TILES_PER_GROUP
PADDED_EDGES = N_TILES * TILE
LAST_TILE = (N_EDGES - 1) // TILE
LAST_ROWS = N_EDGES - LAST_TILE * TILE
SLOTS = 4
ROUNDS = N_GROUPS // SLOTS
WINDOW = 80
N_WINDOWS = -(-N_NODES // WINDOW)

DENSE_K = SLOTS - 1
SRC_BUFFERS = 4
SRC_PITCH = N_NODES + N_NODES % 2
SRC_SHIFT = N_NODES // 2
assert GROUP <= 2048 and SRC_SHIFT < 2048 and N_NODES - SRC_SHIFT < 2048

PULLED = TILES_PER_GROUP - 1
LAST_PULLED = 1
EDGE_SLOTS = 2
MESSAGE_TILES = (range(0, 5), range(5, TILES_PER_GROUP))
assert N_GROUPS % EDGE_SLOTS == 0

PARTS = 125
PART_SPANS = ((0, 112), (112, PARTS))
BLOCKS = N_NODES // PARTS
ROW = FEAT + 1
BANK = 512

CHUNK_BOUNDS = (0, 5, 10, 15, 19, 22, BLOCKS)
CHUNK_COMPLETE = (3, 6, 9, 12, 12, ROUNDS)
CHUNKS = [range(b0, b1) for b0, b1 in zip(CHUNK_BOUNDS, CHUNK_BOUNDS[1:])]
N_CHUNKS = len(CHUNKS)
STARTS = [0] + sorted(set(CHUNK_COMPLETE[:-1]))
SPANS = [(r0, r1, [c for c in range(N_CHUNKS) if CHUNK_COMPLETE[c] == r0])
         for r0, r1 in zip(STARTS, STARTS[1:] + [ROUNDS])]
SELF_TERMS = ((0,), (1,), (2,), (3,), (4, 5))
SELF_SECOND = [chunks[1] for chunks in SELF_TERMS if len(chunks) > 1]
DVE_BLOCKS = 1
EPS = 1e-5

assert N_GROUPS == SLOTS * ROUNDS and BLOCKS * PARTS == N_NODES and LAST_TILE == N_TILES - 1
assert max(len(blocks) for blocks in CHUNKS) * ROW <= BANK

CONSTANT_WIDTHS = (TILE, WINDOW, N_WINDOWS, 1, BLOCKS)


def chunk_blocks(c):
    return slice(CHUNKS[c].start, CHUNKS[c].stop)


def is_pulled(k, last_round):
    return not last_round or k <= LAST_PULLED


def next_group(r, k, ahead):
    return (r, k + ahead) if k + ahead < SLOTS else (r + 1, k + ahead - SLOTS)


def mlp_stages(chunks, k):
    return [(c, stage) for i, c in enumerate(chunks) for stage in range(2) if 2 * i + stage == k]


def chunk_nodes(c):
    return slice(CHUNKS[c].start * PARTS, CHUNKS[c].stop * PARTS)


def half_blocks(c, half):
    blocks = CHUNKS[c]
    middle = blocks.start + (len(blocks) + 1) // 2
    return range(middle, blocks.stop) if half else range(blocks.start, middle)


def gnn_two_layers(nc, x, src, dst, dst_grouped, edge_attr, w_neigh, w_self, w_edge, b_edge,
                   w1, b1, w2, b2, gamma, beta, constants, source_numbers, pulled_sources, out):
    fp32 = mybir.dt.float32
    i32 = mybir.dt.int32
    fp16 = mybir.dt.float16
    bf16 = mybir.dt.bfloat16
    ALU = mybir.AluOpType
    ACT = mybir.ActivationFunctionType
    AX = mybir.AxisListType.X

    tables = [nc.dram_tensor(f"feature_table{layer}", (N_NODES, FEAT), fp32, kind="Internal").ap()
              for layer in range(2)]

    def node_major(array):
        return array.rearrange("(b p) f -> p b f", p=PARTS)

    with ExitStack() as ctx:
        def sb(name, shape, dt=fp32):
            return ctx.enter_context(nc.sbuf_tensor(name, shape, dt))

        def sem(name):
            return ctx.enter_context(nc.semaphore(name))

        x_sb = sb("x_sb", [PARTS, BLOCKS, FEAT])
        h1_parts = sb("h1_parts", [PARTS, BLOCKS, 3, FEAT], bf16)
        x_mid = sb("x_mid", [PARTS, BLOCKS, FEAT])
        h = sb("h", [PARTS, BLOCKS, FEAT])
        block_stats = sb("block_stats", [PARTS, BLOCKS, 6])
        mean_var = sb("mean_var", [PARTS, BLOCKS, 2])
        rstd = sb("rstd", [PARTS, BLOCKS])
        neg_mean_rstd = sb("neg_mean_rstd", [PARTS, BLOCKS])
        degree = sb("degree", [PARTS, BLOCKS])
        hT = sb("hT", [FEAT, N_NODES])
        h_parts_space = sb("h_parts_space", [TILE, 3 * BLOCKS * ROW + 1], bf16)
        r1T = h_parts_space[0:FEAT, 0:2 * N_NODES].bitcast(fp32)
        h2T_space = sb("h2T_space", [TILE, N_NODES])
        h2T = h2T_space[0:FEAT]
        h_rest = h2T_space[0:PARTS, 0:BLOCKS * FEAT].rearrange("p (b f) -> p b f", f=FEAT)
        sums = [sb(f"sums{layer}", [ROW, N_NODES + WINDOW]) for layer in range(2)]

        src_idx = sb("src_idx", [TILE, N_TILES + SLOTS * TILES_PER_GROUP], i32)
        slot_idx = sb("slot_idx", [TILE, SLOTS, TILES_PER_GROUP], i32)
        dst_i = sb("dst_i", [TILE, N_TILES], i32)
        dst_f = sb("dst_f", [TILE, N_TILES])
        dst_rel = sb("dst_rel", [TILE, N_TILES])
        dst_pass = sb("dst_pass", [TILE, TILES_PER_GROUP])
        grp_i = sb("grp_i", [N_GROUPS, GROUP], i32)
        grp_min = sb("grp_min", [N_GROUPS, 1])
        grp_max = sb("grp_max", [N_GROUPS, 1])
        grp_early = sb("grp_early", [N_GROUPS, 1])
        grp_odd = sb("grp_odd", [N_GROUPS, 1])
        grp_diag = sb("grp_diag", [N_GROUPS, N_GROUPS])
        starts_i = sb("starts_i", [1, N_GROUPS], i32)
        odd_i = sb("odd_i", [1, 1], i32)
        constants_sb = sb("constants_sb", [TILE, sum(CONSTANT_WIDTHS)])
        identity, columns_f, windows_f, complete, own_nodes = (
            constants_sb[:, sum(CONSTANT_WIDTHS[:i]):sum(CONSTANT_WIDTHS[:i + 1])] for i in range(len(CONSTANT_WIDTHS)))
        ones = sb("ones", [N_GROUPS, TILE])

        rows = sb("rows", [TILE, SLOTS, TILES_PER_GROUP, ROW])
        onehot = [sb(f"onehot{i}", [TILE, TILES_PER_GROUP, WINDOW]) for i in range(DENSE_K)]
        message = sb("message", [TILE, TILES_PER_GROUP, FEAT])
        edges = sb("edges", [EDGE_FEAT + 1, EDGE_SLOTS, GROUP])
        src_f = sb("src_f", [TILE, N_TILES])
        src_numbers = sb("src_numbers", [TILE, SRC_PITCH], fp16)
        src_onehot = sb("src_onehot", [TILE, SRC_BUFFERS, SRC_PITCH], fp16)
        dst_onehot = sb("dst_onehot", [TILE, TILES_PER_GROUP, WINDOW], fp16)
        pulled_src = sb("pulled_src", [PARTS, SLOTS, TILE], i32)
        pull_onehot = src_onehot[0:PARTS].rearrange("p t n -> p (t n)")[:, 0:2 * BLOCKS * TILE].rearrange(
            "p (i b e) -> p i b e", i=2, b=BLOCKS)
        identity_h = sb("identity_h", [WINDOW, WINDOW], fp16)
        counts = sb("counts", [WINDOW, N_NODES], fp16)
        countsT = sb("countsT", [PARTS, BLOCKS, WINDOW], fp16)
        h_parts = h_parts_space[0:PARTS, 0:3 * BLOCKS * ROW].rearrange("p (b i f) -> p b i f", i=3, f=ROW)
        dense_sum = sb("dense_sum", [WINDOW, ROW])
        gate_in = sb("gate_in", [1, 1], i32)
        gate_out = sb("gate_out", [1, 1], i32)

        w_neigh_sb = sb("w_neigh_sb", [ROW, ROW])
        w_self_sb = sb("w_self_sb", [FEAT, FEAT])
        w_edge_wide = sb("w_edge_wide", [EDGE_FEAT + 1, 3 * FEAT])
        w_edge_sb = w_edge_wide[:, 0:FEAT]
        w1_sb = sb("w1_sb", [FEAT, FEAT])
        w2_sb = sb("w2_sb", [FEAT, FEAT])
        vectors = sb("vectors", [FEAT, 4])
        bn_parts = sb("bn_parts", [FEAT, 2 * N_CHUNKS, 6])
        bn = sb("bn", [FEAT, 2])
        bn_scale = sb("bn_scale", [FEAT, 1])
        bn_shift = sb("bn_shift", [FEAT, 1])
        eps_col = sb("eps_col", [TILE, 1])
        first_root = sb("first_root", [1, 1])

        psum = ctx.enter_context(nc.psum_tensor("psum", [TILE, 8, BANK], fp32))
        window_ps = [psum[:, 0, first:first + WINDOW] for first in (0, 2 * TILE, 3 * TILE, TILE)]
        starts_ps = psum[:, 0, TILE:TILE + N_GROUPS]
        odd_ps = psum[:, 0, TILE + N_GROUPS:TILE + N_GROUPS + 1]
        edge_ps = [[psum[:, bank + half, 0:len(MESSAGE_TILES[half]) * FEAT].rearrange("p (t f) -> p t f", f=FEAT)
                    for half in range(2)] for bank in (1, 3)]
        pulled_cols = slice((PULLED - MESSAGE_TILES[1].start) * FEAT, (PULLED - MESSAGE_TILES[1].start + 3) * FEAT)
        pulled_ps = [psum[:, bank + 1, pulled_cols].rearrange("p (i f) -> p i f", i=3) for bank in (1, 3)]
        assert pulled_cols.stop <= BANK

        def node_ps(bank, c, width):
            bank = psum[0:PARTS, bank, :]
            return bank[:, 0:len(CHUNKS[c]) * width].rearrange("p (b f) -> p b f", f=width)

        def half_columns(c, half):
            blocks = half_blocks(c, half)
            return slice(blocks.start * PARTS, blocks.stop * PARTS)

        def half_ps(bank, c, half):
            return psum[0:FEAT, bank, 0:len(half_blocks(c, half)) * PARTS]

        counts_ps = psum[0:WINDOW, 1:8, :].rearrange("d b n -> d (b n)")
        T_BLOCKS = 2 * BANK // WINDOW
        countsT_chunks = [(b, min(b + T_BLOCKS, BLOCKS)) for b in range(0, BLOCKS, T_BLOCKS)]

        def countsT_ps(n):
            b0, b1_ = countsT_chunks[n]
            bank = psum[0:PARTS, 1 + n, :].bitcast(fp16)
            return bank[:, 0:(b1_ - b0) * WINDOW].rearrange("s (b d) -> s b d", d=WINDOW)

        dense_ps = psum[0:WINDOW, 7, BANK - 3 * ROW:]
        assert len(countsT_chunks) < 7 and N_NODES <= 7 * BANK - 3 * ROW

        SUMS_BANK = 4
        RESULT_BANK = 2
        mm1_banks, mm2_banks = (5, 6), (7, 5)

        def place(layer, k):
            return k if layer == 0 else k % 2

        def self_bank(c):
            return 5 if c in SELF_SECOND else 6

        def transposed_ps(layer, c, half):
            if layer == 1:
                return half_ps((3, 5, 6, 7)[(2 * c + half) % 4], c, half)
            if c in SELF_SECOND:
                first = half * len(half_blocks(c, 0)) * PARTS
                return psum[0:FEAT, 5, first:first + len(half_blocks(c, half)) * PARTS]
            return half_ps(5 + half, c, half)

        x_loaded = [sem(f"x_loaded{c}") for c in range(N_CHUNKS)]
        src_loaded = sem("src_loaded")
        dst_loaded = sem("dst_loaded")
        grp_loaded = sem("grp_loaded")
        weights_loaded = sem("weights_loaded")
        edges_loaded = [sem(f"edges_loaded{k}") for k in range(EDGE_SLOTS)]
        pulled_src_loaded = [sem(f"pulled_src_loaded{k}") for k in range(SLOTS)]
        pull_onehots = sem("pull_onehots")
        h1_part = [sem(f"h1_part{i}") for i in range(3)]
        h1_rest = [sem(f"h1_rest{i}") for i in range(2)]
        gathered = [[sem(f"gathered{layer}_{k}") for k in range(SLOTS)] for layer in range(2)]
        constants_loaded = sem("constants_loaded")
        eps_made = sem("eps_made")
        consts_made = sem("consts_made")
        dve_step = sem("dve_step")
        gate_passed = sem("gate_passed")
        slot_ready = sem("slot_ready")
        var_ready = sem("var_ready")
        std_ready = sem("std_ready")
        std_inv = sem("std_inv")
        h_dve = sem("h_dve")
        h_act = sem("h_act")
        table_written = [sem(f"table_written{layer}") for layer in range(2)]
        transposed = sem("transposed")
        hT_copied = sem("hT_copied")
        self_done = sem("self_done")
        self_added = sem("self_added")
        identity_copied = sem("identity_copied")
        diag_ready = sem("diag_ready")
        starts_done = sem("starts_done")
        routing_ready = sem("routing_ready")
        onehot_ready = [sem(f"onehot_ready{layer}") for layer in range(2)]
        scattered = [sem(f"scattered{layer}") for layer in range(2)]
        numbers_loaded = sem("numbers_loaded")
        src_onehot_ready = sem("src_onehot_ready")
        src_onehot_free = sem("src_onehot_free")
        dst_onehot_ready = sem("dst_onehot_ready")
        counted = sem("counted")
        counts_copied = sem("counts_copied")
        countsT_done = sem("countsT_done")
        countsT_copied = sem("countsT_copied")
        window_added = sem("window_added")
        dense_done = sem("dense_done")
        dense_reduced = sem("dense_reduced")
        part_made = sem("part_made")
        rest_made = sem("rest_made")
        pass_shifted = sem("pass_shifted")
        pass_onehot = sem("pass_onehot")
        pass_scattered = sem("pass_scattered")
        sums_cleared = sem("sums_cleared")
        sums_done = sem("sums_done")
        neigh_done = sem("neigh_done")
        node_sums_read = sem("node_sums_read")
        edge_terms = sem("edge_terms")
        summed = sem("summed")
        message_ready = sem("message_ready")
        hT_summed = sem("hT_summed")
        mm1_done = sem("mm1_done")
        r1_ready = sem("r1_ready")
        mm2_done = sem("mm2_done")
        h2_ready = sem("h2_ready")
        bn_var = sem("bn_var")
        bn_std = sem("bn_std")
        bn_ready = sem("bn_ready")
        resultT_ready = sem("resultT_ready")
        result_done = sem("result_done")
        out_ready = sem("out_ready")
        out_written = sem("out_written")

        b1_col, b2_col, gamma_col, beta_col = (vectors[:, i:i + 1] for i in range(4))
        N_WEIGHTS = 10

        block = ctx.enter_context(nc.Block())

        @block.sync
        def _(sp):
            for c in range(N_CHUNKS):
                for p0, p1 in PART_SPANS:
                    sp.dma_start(x_sb[p0:p1, chunk_blocks(c)],
                                 node_major(x)[p0:p1, chunk_blocks(c)]).then_inc(x_loaded[c], 16)
            sp.dma_start(src_numbers[:], source_numbers.to_broadcast([TILE, SRC_PITCH])
                         ).then_inc(numbers_loaded, 16)
            for layer in range(2):
                for c in range(N_CHUNKS):
                    sp.wait_ge(h_dve, layer * N_CHUNKS + c + 1)
                    sp.wait_ge(h_act, layer * N_CHUNKS + c + 1)
                    for p0, p1 in PART_SPANS:
                        sp.dma_start(node_major(tables[layer])[p0:p1, chunk_blocks(c)],
                                     h[p0:p1, chunk_blocks(c)]).then_inc(table_written[layer], 16)
                if layer == 0:
                    for k in range(EDGE_SLOTS):
                        sp.dma_start(edges[0:EDGE_FEAT, k, :], edge_attr[k]).then_inc(edges_loaded[k], 16)
            with sp.Fori(1, N_GROUPS // EDGE_SLOTS) as n:
                for k in range(EDGE_SLOTS):
                    sp.wait_ge(edge_terms, (n - 1) * EDGE_SLOTS + k + 1)
                    sp.dma_start(edges[0:EDGE_FEAT, k, :],
                                 edge_attr[bass.ds(n * EDGE_SLOTS + k, 1)].rearrange("g f e -> (g f) e")
                                 ).then_inc(edges_loaded[k], 16)
            for c in range(N_CHUNKS):
                sp.wait_ge(out_ready, c + 1)
                for p0, p1 in PART_SPANS:
                    sp.dma_start(node_major(out)[p0:p1, chunk_blocks(c)],
                                 x_mid[p0:p1, chunk_blocks(c)]).then_inc(out_written, 16)
            for written in (*table_written, out_written):
                sp.wait_ge(written, 32 * N_CHUNKS)

        @block.gpsimd
        def _(pool):
            nc.gpsimd.memset(gate_in[:], 0).then_inc(gate_passed, 1)
            pool.wait_ge(gate_passed, 1)
            nc.gpsimd.memset(edges[EDGE_FEAT:, :, :], 1.0).then_inc(sums_cleared, 1)
            for layer in range(2):
                pool.wait_ge(sums_cleared, layer + 1)
                nc.gpsimd.memset(sums[layer][:], 0.0).then_inc(sums_cleared, 1)

            def gather_group(layer, r, k, tiles=TILES_PER_GROUP):
                if k % 2 == 0:
                    pool.wait_ge(gate_passed, (layer * N_GROUPS + r * SLOTS + k) // 2 + 1)
                    pool.wait_ge(slot_ready, layer * N_GROUPS + r * SLOTS + k + 2)
                    nc.gpsimd.tensor_tensor(gate_out[:], gate_in[:], gate_in[:],
                                            ALU.add).then_inc(gate_passed, 1)
                for j in range(tiles):
                    nc.gpsimd.indirect_dma_start(
                        out=rows[:, k, j, 0:FEAT], out_offset=None, in_=tables[layer],
                        in_offset=bass.IndirectOffsetOnAxis(ap=slot_idx[:, k, j:j + 1], axis=0),
                    ).then_inc(gathered[layer][k], 16)

            pool.wait_ge(table_written[0], 32 * N_CHUNKS)
            for k in range(DENSE_K):
                gather_group(0, 0, k)
            pool.wait_ge(routing_ready, 1)
            odd = pool.value_load(odd_i[0:1, 0:1], min_val=0, max_val=2 * N_GROUPS)
            with pool.If(odd):
                gather_group(0, 0, DENSE_K)
                with pool.Fori(1, ROUNDS) as r:
                    for k in range(SLOTS):
                        gather_group(0, r, k)
            with pool.Else():
                with pool.Fori(1, ROUNDS) as r:
                    for k in range(DENSE_K):
                        gather_group(0, r, k)
            pool.wait_ge(table_written[1], 32 * N_CHUNKS)
            with pool.If(odd):
                with pool.Fori(0, ROUNDS) as r:
                    for k in range(SLOTS):
                        gather_group(1, r, k)
            with pool.Else():
                with pool.Fori(0, ROUNDS - 1) as r:
                    for k in range(SLOTS):
                        gather_group(1, r, k, PULLED)
                for k in range(SLOTS):
                    gather_group(1, ROUNDS - 1, k, PULLED if is_pulled(k, True) else TILES_PER_GROUP)

        @block.vector
        def _(dve):
            steps = [0]

            def chained(instruction):
                steps[0] += 1
                instruction.then_inc(dve_step, 1)
                dve.wait_ge(dve_step, steps[0])

            def statistics(features, c):
                blocks = CHUNKS[c]
                for b in blocks:
                    last = nc.vector.bn_stats(block_stats[:, b], features[:, b])
                chained(last)
                for b in blocks:
                    last = nc.vector.bn_aggr(mean_var[:, b], block_stats[:, b])
                last.then_inc(var_ready, 1)

            def normalise(features, c, layer):
                here = chunk_blocks(c)
                dve.wait_ge(std_ready, layer * N_CHUNKS + c + 1)
                chained(nc.vector.reciprocal(rstd[:, here], rstd[:, here]))
                nc.vector.scalar_tensor_tensor(neg_mean_rstd[:, here], mean_var[:, here, 0], -1.0, rstd[:, here],
                                               ALU.mult, ALU.mult).then_inc(std_inv, 1)
                own = CHUNKS[c][:DVE_BLOCKS]
                for b in own:
                    last = nc.vector.tensor_scalar(h[:, b], features[:, b], mean_var[:, b, 0:1], 0.0,
                                                   ALU.subtract, ALU.max)
                chained(last)
                for b in own:
                    last = nc.vector.tensor_scalar(h[:, b], h[:, b], rstd[:, b:b + 1], None, ALU.mult)
                last.then_inc(h_dve, 1)

            nc.vector.memset(eps_col[:], EPS).then_inc(eps_made, 1)
            nc.vector.memset(ones[:], 1.0)
            nc.vector.memset(w_edge_wide[:, FEAT:], 0.0)
            nc.vector.memset(rows[:, :, :, FEAT:ROW], 1.0)
            for i in range(3):
                nc.vector.memset(h_parts[:, :, i, FEAT:ROW], 1.0 if i == 0 else 0.0)
            chained(nc.vector.memset(w_neigh_sb[:], 0.0))
            nc.vector.memset(w_neigh_sb[FEAT:ROW, FEAT:ROW], 1.0)
            nc.vector.drain().then_inc(src_onehot_free, SRC_BUFFERS)
            nc.vector.drain().then_inc(consts_made, 1)
            dve.wait_ge(grp_loaded, 16)
            nc.vector.tensor_reduce(grp_min[:], grp_i[:], AX, ALU.min)
            for c in range(N_CHUNKS):
                dve.wait_ge(x_loaded[c], 32)
                statistics(x_sb, c)
                if c > 0:
                    normalise(x_sb, c - 1, 0)
            normalise(x_sb, N_CHUNKS - 1, 0)

            dve.wait_ge(src_loaded, 32)
            nc.vector.tensor_copy(slot_idx[:].rearrange("p s t -> p (s t)"),
                                  src_idx[:, 0:SLOTS * TILES_PER_GROUP]).then_inc(slot_ready, SLOTS)

            chained(nc.vector.tensor_reduce(grp_max[:], grp_i[:], AX, ALU.max))
            dve.wait_ge(constants_loaded, 16)
            nc.vector.tensor_scalar(grp_diag[:], identity[0:N_GROUPS, 0:N_GROUPS], grp_min[:], None,
                                    ALU.mult).then_inc(diag_ready, 1)
            nc.vector.tensor_tensor(grp_early[:], grp_min[:], complete[0:N_GROUPS], ALU.is_lt)
            chained(nc.vector.tensor_tensor(grp_odd[:], grp_max[:], grp_min[:], ALU.subtract))
            chained(nc.vector.tensor_scalar(grp_odd[:], grp_odd[:], float(WINDOW), None, ALU.is_ge))
            nc.vector.tensor_tensor(grp_odd[:], grp_odd[:], grp_early[:], ALU.add).then_inc(diag_ready, 1)

            dve.wait_ge(dst_loaded, 16)
            nc.vector.tensor_scalar(src_f[:], src_idx[:, 0:N_TILES], float(SRC_SHIFT), None, ALU.subtract)
            chained(nc.vector.tensor_copy(dst_f[:], dst_i[:]))
            chained(nc.vector.memset(dst_f[:, LAST_TILE:], -1e6))
            chained(nc.vector.tensor_copy(dst_f[0:LAST_ROWS, LAST_TILE:], dst_i[0:LAST_ROWS, LAST_TILE:]))
            dve.wait_ge(starts_done, 1)
            nc.vector.tensor_tensor(
                dst_rel[:].rearrange("p (g t) -> p g t", t=TILES_PER_GROUP),
                dst_f[:].rearrange("p (g t) -> p g t", t=TILES_PER_GROUP),
                starts_ps.rearrange("p (g o) -> p g o", o=1).to_broadcast(
                    [TILE, N_GROUPS, TILES_PER_GROUP]), ALU.subtract)
            nc.vector.tensor_copy(starts_i[:], starts_ps[0:1])
            chained(nc.vector.tensor_copy(odd_i[:], odd_ps[0:1]))
            nc.vector.drain().then_inc(routing_ready, 1)

            def make_onehot(dst_of_edge, made):
                shape = [TILE, TILES_PER_GROUP, WINDOW]
                return nc.vector.tensor_tensor(
                    made[:], columns_f.rearrange("p (o n) -> p o n", o=1).to_broadcast(shape),
                    dst_of_edge.rearrange("p (t o) -> p t o", o=1).to_broadcast(shape), ALU.is_equal)

            def source_onehot(tile, n):
                return nc.vector.tensor_scalar(src_onehot[:, n % SRC_BUFFERS], src_numbers[:], src_f[:, tile], None,
                                               ALU.is_equal).then_inc(src_onehot_ready, 1)

            make_onehot(dst_rel[:, DENSE_K * TILES_PER_GROUP:SLOTS * TILES_PER_GROUP],
                        dst_onehot).then_inc(dst_onehot_ready, 1)
            dve.wait_ge(numbers_loaded, 16)
            for j in range(SRC_BUFFERS):
                tile = DENSE_K * TILES_PER_GROUP + j
                source_onehot(slice(tile, tile + 1), j)

            def add_self_terms(chunks):
                for c in chunks:
                    dve.wait_ge(self_done, c + 1)
                    nc.vector.tensor_tensor(x_mid[:, chunk_blocks(c)], x_sb[:, chunk_blocks(c)],
                                            node_ps(self_bank(c), c, FEAT), ALU.add).then_inc(self_added, 1)

            def add_edge_terms(r, k, pulled, general):
                group = r * SLOTS + k
                tiles = PULLED if pulled else TILES_PER_GROUP
                rows_before = r * 16 * (TILES_PER_GROUP if general else PULLED)
                dve.wait_ge(gathered[1][k], rows_before + 16 * tiles)
                dve.wait_ge(edge_terms, group + 1)
                parity = 0 if general else k % 2
                for half in range(2):
                    here = slice(MESSAGE_TILES[half].start, min(MESSAGE_TILES[half].stop, tiles))
                    added = nc.vector.tensor_tensor(message[:, here], rows[:, k, here, 0:FEAT],
                                                    edge_ps[parity][half][:, 0:here.stop - here.start], ALU.add)
                    if half == 1 and pulled:
                        added = nc.vector.tensor_reduce(message[:, PULLED],
                                                        pulled_ps[parity].rearrange("e i f -> e f i"), AX, ALU.add)
                    added.then_inc(summed, 1)

            def make_pull_onehot(r, k):
                dve.wait_ge(pulled_src_loaded[k], (r + 1) * 16)
                shape = [PARTS, BLOCKS, TILE]
                nc.vector.tensor_tensor(
                    pull_onehot[:, k % 2],
                    pulled_src[:, k, :].rearrange("p (o e) -> p o e", o=1).to_broadcast(shape),
                    own_nodes[0:PARTS].rearrange("p (b o) -> p b o", o=1).to_broadcast(shape),
                    ALU.is_equal).then_inc(pull_onehots, 1)

            def split_h1(i, c):
                here = chunk_blocks(c)
                dve.wait_ge(h1_part[i], c + 1)
                nc.vector.tensor_tensor(h_rest[:, here], (h, h_rest)[i][:, here], h1_parts[:, here, i],
                                        ALU.subtract).then_inc(h1_rest[i], 1)

            def add_window(layer, start, made):
                window = sums[layer][:, bass.ds(start, WINDOW)]
                return nc.vector.tensor_tensor(window, window, made[0:ROW], ALU.add)

            def dense_onehots(r, tiles):
                group = r * SLOTS + DENSE_K
                if 0 in tiles:
                    make_onehot(dst_rel[:, bass.ds(group * TILES_PER_GROUP, TILES_PER_GROUP)],
                                dst_onehot).then_inc(dst_onehot_ready, 1)
                for j in tiles:
                    dve.wait_ge(src_onehot_free, r * TILES_PER_GROUP + j + 1)
                    source_onehot(bass.ds(group * TILES_PER_GROUP + j, 1), j)

            def split_features(i):
                dve.wait_ge(part_made, i + 1)
                nc.vector.tensor_tensor(h_rest[:], (h, h_rest)[i][:], h_parts[:, :, i, 0:FEAT],
                                        ALU.subtract).then_inc(rest_made, 1)

            def dense_round(r, span=None):
                begins = span is not None
                first, last = begins and r == 0, begins and r == ROUNDS - 1
                if first:
                    group_onehot(0, r, 0)
                    group_onehot(0, r, 1)
                    dense_onehots(r, range(SRC_BUFFERS, SRC_BUFFERS + 1))
                    split_features(0)
                    dense_onehots(r, range(SRC_BUFFERS + 1, TILES_PER_GROUP))
                    split_features(1)
                else:
                    dense_onehots(r, range(SRC_BUFFERS, TILES_PER_GROUP))
                    group_onehot(0, r, 0)
                    group_onehot(0, r, 1)
                    add_late_windows(r - 1)
                    if begins:
                        complete_sums()
                scatter_group(0, r, 0, general=False, first=first)
                group_onehot(0, r, 2)
                chunks = SPANS[span][2] if begins else []
                for c in chunks[:1]:
                    update_features(c)
                scatter_group(0, r, 1, general=False)
                for c in chunks[:1]:
                    finish_features(c, general=False)
                if begins:
                    add_self_terms(SELF_TERMS[span][:1])
                for c in chunks[1:]:
                    finish_chunk(c, general=False)
                if not last and not chunks:
                    dense_onehots(r + 1, range(SRC_BUFFERS))
                dve.wait_ge(dense_done, r + 1)
                nc.vector.tensor_reduce(dense_sum[:], dense_ps.rearrange("d (i f) -> d f i", i=3), AX,
                                        ALU.add).then_inc(dense_reduced, 1)
                if not last and chunks:
                    dense_onehots(r + 1, range(SRC_BUFFERS))
                nc.vector.drain().then_inc(slot_ready, 1)
                split_chunks(chunks, (0,) if last else (0, 1))
                if begins:
                    add_self_terms(SELF_TERMS[span][1:])

            def split_chunks(chunks, steps_to_take=(0, 1)):
                for i in steps_to_take:
                    for c in chunks:
                        split_h1(i, c)

            def add_late_windows(r):
                start = group_start(r * SLOTS + DENSE_K)
                dve.wait_ge(scattered[0], (r + 1) * DENSE_K)
                dve.wait_ge(window_added, r * SLOTS + 2)
                add_window(0, start, window_ps[DENSE_K]).then_inc(window_added, 1)
                scatter_group(0, r, DENSE_K - 1, general=False)

            def refill_slot(group, k):
                nc.vector.tensor_copy(
                    slot_idx[:, k, :],
                    src_idx[:, bass.ds((group + SLOTS) * TILES_PER_GROUP, TILES_PER_GROUP)]
                ).then_inc(slot_ready, 1)

            def group_onehot(layer, r, k):
                group_tiles = bass.ds((r * SLOTS + k) * TILES_PER_GROUP, TILES_PER_GROUP)
                make_onehot(dst_rel[:, group_tiles], onehot[place(layer, k)]).then_inc(onehot_ready[layer], 1)

            def group_start(group):
                return dve.value_load(starts_i[0:1, bass.ds(group, 1)], min_val=0, max_val=N_NODES - 1)

            def message_group(r, k, last_round=False, hidden=None):
                group = r * SLOTS + k
                start = group_start(group)
                add_edge_terms(r, k, is_pulled(k, last_round), general=False)
                refill_slot(group, k)
                if not last_round:
                    make_pull_onehot(*next_group(r, k, 2))
                if hidden is not None:
                    add_hidden(hidden)
                if k < SLOTS - 1 or not last_round:
                    group_onehot(1, *next_group(r, k, 1))
                dve.wait_ge(scattered[1], group + 1)
                add_window(1, start, window_ps[place(1, k)])

            def scatter_group(layer, r, k, general, first=False):
                group = r * SLOTS + k
                group_tiles = bass.ds(group * TILES_PER_GROUP, TILES_PER_GROUP)
                if not general:
                    start = group_start(group)
                if layer == 1:
                    add_edge_terms(r, k, pulled=False, general=True)
                if not general:
                    dve.wait_ge(scattered[0], r * DENSE_K + k + 1)
                    if not first:
                        dve.wait_ge(window_added, r * SLOTS + (3 if k == 2 else k))
                    add_window(0, start, window_ps[place(0, k)]).then_inc(window_added, 1)
                else:
                    with dve.Fori(0, N_WINDOWS) as w:
                        passes = (layer * N_GROUPS + group) * N_WINDOWS + w
                        nc.vector.tensor_tensor(
                            dst_pass[:], dst_f[:, group_tiles],
                            windows_f[:, bass.ds(w, 1)].to_broadcast([TILE, TILES_PER_GROUP]),
                            ALU.subtract).then_inc(pass_shifted, 1)
                        dve.wait_ge(pass_shifted, passes + 1)
                        make_onehot(dst_pass[:], onehot[0]).then_inc(pass_onehot, 1)
                        dve.wait_ge(pass_scattered, passes + 1)
                        add_window(layer, w * WINDOW, window_ps[0])
                refill_slot(group, k)

            def update_features(c):
                here = chunk_blocks(c)
                sums_ps = node_ps(SUMS_BANK, c, ROW)
                dve.wait_ge(neigh_done, c + 1)
                chained(nc.vector.tensor_scalar(degree[:, here], sums_ps[:, :, FEAT], 1.0, None, ALU.max))
                chained(nc.vector.reciprocal(degree[:, here], degree[:, here]))
                for i, b in enumerate(CHUNKS[c]):
                    last = nc.vector.scalar_tensor_tensor(
                        x_mid[:, b], sums_ps[:, i, 0:FEAT], degree[:, b:b + 1],
                        x_mid[:, b], ALU.mult, ALU.add)
                chained(last)
                nc.vector.drain().then_inc(node_sums_read, 1)
                statistics(x_mid, c)

            def finish_features(c, general):
                if c == 0:
                    dve.wait_ge(table_written[0], 32 * N_CHUNKS)
                    if not general:
                        dve.wait_ge(part_made, 3)
                dve.wait_ge(transposed, 2 * (c + 1))
                normalise(x_mid, c, 1)

            def finish_chunk(c, general):
                update_features(c)
                finish_features(c, general)

            def add_aggregate(c):
                chained(nc.vector.drain())
                dve.wait_ge(hT_copied, 4 * N_CHUNKS)
                here = chunk_nodes(c)
                nc.vector.tensor_tensor(hT[:, here], hT[:, here], sums[1][0:FEAT, here],
                                        ALU.add).then_inc(hT_summed, 1)

            def add_hidden(c):
                for half in range(2):
                    dve.wait_ge(mm2_done, 2 * c + half + 1)
                    cols = h2T[:, half_columns(c, half)]
                    chained(nc.vector.tensor_scalar(cols, half_ps(mm2_banks[half], c, half), b2_col, None, ALU.add))
                    nc.vector.bn_stats(bn_parts[:, 2 * c + half, :], cols).then_inc(h2_ready, 1)

            odd = dve.value_load(odd_i[0:1, 0:1], min_val=0, max_val=2 * N_GROUPS)
            dve.wait_ge(weights_loaded, 16 * N_WEIGHTS)
            dve.wait_ge(sums_cleared, 3)

            def complete_sums():
                chained(nc.vector.drain())
                nc.vector.drain().then_inc(sums_done, 1)

            def run_layer(layer, general):
                if general:
                    if layer == 0:
                        add_self_terms(range(N_CHUNKS))
                    with dve.Fori(0, ROUNDS) as r:
                        for k in range(SLOTS):
                            scatter_group(layer, r, k, general=True)
                    if layer == 0:
                        for _ in SPANS:
                            complete_sums()
                    for c in range(N_CHUNKS):
                        if layer == 0:
                            finish_chunk(c, general)
                        else:
                            add_aggregate(c)
                            add_hidden(c)
                elif layer == 0:
                    for span, (r0, r1, chunks) in enumerate(SPANS):
                        dense_round(r0, span)
                        if r0 + 1 < r1:
                            with dve.Fori(r0 + 1, r1) as r:
                                dense_round(r)
                    add_late_windows(ROUNDS - 1)
                    complete_sums()
                    split_chunks(chunks, (1,))
                    finish_chunk(N_CHUNKS - 1, general)
                    group_onehot(1, 0, 0)
                    for k in range(2):
                        make_pull_onehot(0, k)
                    split_chunks([N_CHUNKS - 1])
                else:
                    for r0, r1, chunks in SPANS:
                        for c in chunks:
                            add_aggregate(c)
                        for k in range(SLOTS):
                            hidden = [c for c, stage in mlp_stages(chunks, k - 1) if stage == 1]
                            message_group(r0, k, r0 == ROUNDS - 1, *hidden)
                        if r0 + 1 < r1:
                            with dve.Fori(r0 + 1, r1) as r:
                                for k in range(SLOTS):
                                    message_group(r, k)
                    for c, stage in mlp_stages(chunks, SLOTS - 1):
                        add_hidden(c)
                    add_aggregate(N_CHUNKS - 1)
                    add_hidden(N_CHUNKS - 1)

            for layer in range(2):
                before = steps[0]
                with dve.If(odd):
                    run_layer(layer, general=True)
                after = steps[0]
                steps[0] = before
                with dve.Else():
                    run_layer(layer, general=False)
                assert steps[0] == after

            dve.wait_ge(h2_ready, 2 * N_CHUNKS)
            nc.vector.bn_aggr(bn[:], bn_parts[:].rearrange("f c s -> f (c s)")).then_inc(bn_var, 1)
            dve.wait_ge(bn_std, 1)
            chained(nc.vector.reciprocal(bn_scale[:], bn_scale[:]))
            chained(nc.vector.tensor_tensor(bn_scale[:], bn_scale[:], gamma_col, ALU.mult))
            chained(nc.vector.tensor_tensor(bn_shift[:], bn[:, 0:1], bn_scale[:], ALU.mult))
            nc.vector.tensor_tensor(bn_shift[:], beta_col, bn_shift[:], ALU.subtract).then_inc(bn_ready, 1)
            for c in range(N_CHUNKS):
                dve.wait_ge(result_done, c + 1)
                nc.vector.tensor_tensor(x_mid[:, chunk_blocks(c)], x_mid[:, chunk_blocks(c)],
                                        node_ps(RESULT_BANK + c, c, FEAT), ALU.add).then_inc(out_ready, 1)

        @block.scalar
        def _(act):
            act.dma_start(grp_i[:], dst_grouped).then_inc(grp_loaded, 16)
            act.dma_start(constants_sb[:], constants).then_inc(constants_loaded, 16)
            act.dma_start(src_idx[:, 0:N_TILES], src).then_inc(src_loaded, 16)
            act.dma_start(src_idx[:, N_TILES:], src[:, 0:SLOTS * TILES_PER_GROUP]).then_inc(src_loaded, 16)
            act.dma_start(dst_i[:], dst).then_inc(dst_loaded, 16)

            def deviations(layer, c):
                act.wait_ge(var_ready, layer * N_CHUNKS + c + 1)
                nc.scalar.activation(rstd[:, chunk_blocks(c)], mean_var[:, chunk_blocks(c), 1], ACT.Sqrt,
                                     bias=eps_col[0:PARTS]).then_inc(std_ready, 1)

            def normalise(features, layer, c):
                act.wait_ge(std_inv, layer * N_CHUNKS + c + 1)
                for b in CHUNKS[c][DVE_BLOCKS:]:
                    last = nc.scalar.activation(h[:, b], features[:, b], ACT.Relu, bias=neg_mean_rstd[:, b:b + 1],
                                                scale=rstd[:, b:b + 1])
                last.then_inc(h_act, 1)

            def copy_transposed(layer, chunks):
                for c in chunks:
                    for half in range(2):
                        halves = 2 if layer == 0 and c in SELF_SECOND else half + 1
                        act.wait_ge(transposed, 2 * (layer * N_CHUNKS + c) + halves)
                        nc.scalar.copy(hT[:, half_columns(c, half)],
                                       transposed_ps(layer, c, half)).then_inc(hT_copied, 1)

            act.wait_ge(eps_made, 1)
            nc.scalar.activation(first_root[:], eps_col[0:1], ACT.Sqrt)
            for c in range(N_CHUNKS):
                deviations(0, c)
                normalise(x_sb, 0, c)
            for dst_ap, src_ap in ((w_self_sb[:], w_self), (w_edge_wide[0:EDGE_FEAT, 0:FEAT], w_edge),
                                   (w_edge_wide[EDGE_FEAT:, 0:FEAT], b_edge), (w1_sb[:], w1), (w2_sb[:], w2),
                                   (b1_col, b1), (b2_col, b2), (gamma_col, gamma), (beta_col, beta)):
                act.dma_start(dst_ap, src_ap).then_inc(weights_loaded, 16)
            act.wait_ge(consts_made, 1)
            act.dma_start(w_neigh_sb[0:FEAT, 0:FEAT], w_neigh).then_inc(weights_loaded, 16)
            act.wait_ge(constants_loaded, 16)
            nc.scalar.copy(identity_h[:], identity[0:WINDOW, 0:WINDOW]).then_inc(identity_copied, 1)

            def round_part(i):
                if i > 0:
                    act.wait_ge(rest_made, i)
                nc.scalar.copy(h_parts[:, :, i, 0:FEAT], (h if i == 0 else h_rest)[:]).then_inc(part_made, 1)

            def copy_counts(r, first=False):
                act.wait_ge(counted, r + 1)
                nc.scalar.copy(counts[:], counts_ps[:, 0:N_NODES]).then_inc(counts_copied, 1)
                if first:
                    round_part(2)
                act.wait_ge(countsT_done, r + 1)
                for n, (b0, b1_) in enumerate(countsT_chunks):
                    last = nc.scalar.copy(countsT[:, b0:b1_], countsT_ps(n))
                last.then_inc(countsT_copied, 1)

            def finish_features(c):
                deviations(1, c)
                normalise(x_mid, 1, c)

            def h1_round(i, c):
                here = chunk_blocks(c)
                if i == 0:
                    act.wait_ge(h_dve, N_CHUNKS + c + 1)
                    act.wait_ge(h_act, N_CHUNKS + c + 1)
                else:
                    act.wait_ge(h1_rest[i - 1], c + 1)
                nc.scalar.copy(h1_parts[:, here, i], (h if i == 0 else h_rest)[:, here]).then_inc(h1_part[i], 1)

            act.wait_ge(routing_ready, 1)
            odd = act.value_load(odd_i[0:1, 0:1], min_val=0, max_val=2 * N_GROUPS)
            with act.If(odd):
                copy_transposed(0, range(N_CHUNKS))
                for c in range(N_CHUNKS):
                    finish_features(c)
            with act.Else():
                for k in range(SLOTS):
                    act.dma_start(pulled_src[:, k, :],
                                  pulled_sources[k:k + 1].to_broadcast([PARTS, TILE])
                                  ).then_inc(pulled_src_loaded[k], 16)
                act.wait_ge(h_dve, N_CHUNKS)
                act.wait_ge(h_act, N_CHUNKS)
                for i in range(2):
                    round_part(i)
                for span, (r0, r1, chunks) in enumerate(SPANS):
                    copy_counts(r0, first=(r0 == 0))
                    copy_transposed(0, SELF_TERMS[span][:1])
                    for c in chunks[:1]:
                        finish_features(c)
                        h1_round(0, c)
                    copy_transposed(0, SELF_TERMS[span][1:])
                    for c in chunks[1:]:
                        finish_features(c)
                        h1_round(0, c)
                    for i in (1, 2):
                        for c in chunks:
                            h1_round(i, c)
                    if r0 + 1 < r1:
                        with act.Fori(r0 + 1, r1) as r:
                            copy_counts(r)
                finish_features(N_CHUNKS - 1)
                for i in range(3):
                    h1_round(i, N_CHUNKS - 1)
            act.wait_ge(self_done, N_CHUNKS)
            copy_transposed(1, range(N_CHUNKS))

            def relu_messages(group):
                for half in range(2):
                    tiles = slice(MESSAGE_TILES[half].start, MESSAGE_TILES[half].stop)
                    act.wait_ge(summed, 2 * group + half + 1)
                    nc.scalar.activation(message[:, tiles], message[:, tiles], ACT.Relu).then_inc(message_ready, 1)

            def load_pulled_sources(r, k):
                act.dma_start(pulled_src[:, k, :],
                              pulled_sources[bass.ds(r * SLOTS + k, 1)].to_broadcast([PARTS, TILE])
                              ).then_inc(pulled_src_loaded[k], 16)

            def relu_and_load(r, k, last_round=False):
                relu_messages(r * SLOTS + k)
                if not last_round:
                    act.wait_ge(pull_onehots, r * SLOTS + k + 1)
                    load_pulled_sources(r + 1, k)

            def hidden_layer(c):
                for half in range(2):
                    act.wait_ge(mm1_done, 2 * c + half + 1)
                    nc.scalar.activation(r1T[:, half_columns(c, half)], half_ps(mm1_banks[half], c, half), ACT.Relu,
                                         bias=b1_col).then_inc(r1_ready, 1)

            act.wait_ge(weights_loaded, 16 * N_WEIGHTS)
            with act.If(odd):
                with act.Fori(0, N_GROUPS) as group:
                    relu_messages(group)
                for c in range(N_CHUNKS):
                    hidden_layer(c)
            with act.Else():
                for r0, r1, chunks in SPANS:
                    for k in range(SLOTS):
                        relu_and_load(r0, k, r0 == ROUNDS - 1)
                        for c, stage in mlp_stages(chunks, k):
                            if stage == 0:
                                hidden_layer(c)
                    if r0 + 1 < r1:
                        with act.Fori(r0 + 1, r1) as r:
                            for k in range(SLOTS):
                                relu_and_load(r, k)
                hidden_layer(N_CHUNKS - 1)
                for loaded in pulled_src_loaded:
                    act.wait_ge(loaded, 16 * ROUNDS)
            act.wait_ge(bn_var, 1)
            nc.scalar.activation(bn_scale[:], bn[:, 1:2], ACT.Sqrt, bias=eps_col[0:FEAT]).then_inc(bn_std, 1)
            act.wait_ge(bn_ready, 1)
            act.wait_ge(mm2_done, 2 * N_CHUNKS)
            for c in range(N_CHUNKS):
                here = chunk_nodes(c)
                nc.scalar.activation(r1T[:, here], h2T[:, here], ACT.Relu, bias=bn_shift[:],
                                     scale=bn_scale[:]).then_inc(resultT_ready, 1)

        @block.tensor
        def _(pe):
            def transpose_h(layer, c):
                pe.wait_ge(h_dve, layer * N_CHUNKS + c + 1)
                pe.wait_ge(h_act, layer * N_CHUNKS + c + 1)
                for half in range(2):
                    if layer == 1 and c >= 2:
                        pe.wait_ge(hT_copied, 2 * (N_CHUNKS + c - 2) + half + 1)
                    turned = transposed_ps(layer, c, half)
                    for j, b in enumerate(half_blocks(c, half)):
                        last = nc.tensor.transpose(turned[:, j * PARTS:(j + 1) * PARTS], h[:, b, :],
                                                   identity[0:PARTS, 0:PARTS])
                    last.then_inc(transposed, 1)

            pe.wait_ge(constants_loaded, 16)
            pe.wait_ge(consts_made, 1)
            pe.wait_ge(diag_ready, 2)
            nc.tensor.matmul(starts_ps, ones[:], grp_diag[:], start=True, stop=True)
            nc.tensor.matmul(odd_ps, ones[:], grp_odd[:], start=True, stop=True).then_inc(starts_done, 1)

            def transpose_for_self(c):
                if c in SELF_SECOND:
                    pe.wait_ge(hT_copied, 2 * c)
                elif c > 0:
                    pe.wait_ge(self_added, c)
                transpose_h(0, c)

            def self_term(c):
                pe.wait_ge(weights_loaded, 16 * N_WEIGHTS)
                pe.wait_ge(hT_copied, 2 * (c + 1))
                for j, b in enumerate(CHUNKS[c]):
                    last = nc.tensor.matmul(node_ps(self_bank(c), c, FEAT)[:, j, :],
                                            hT[:, b * PARTS:(b + 1) * PARTS], w_self_sb[:],
                                            start=True, stop=True)
                last.then_inc(self_done, 1)

            def scatter(width, lhs, here, counter, later):
                for j in range(TILES_PER_GROUP):
                    if j in later:
                        pe.wait_ge(*later[j])
                    last = nc.tensor.matmul(window_ps[here][0:width], lhs(j), onehot[here][:, j, :],
                                            start=(j == 0), stop=(j == TILES_PER_GROUP - 1))
                last.then_inc(counter, 1)

            def edge_products(r, k, pulled, general):
                pe.wait_ge(edges_loaded[k % EDGE_SLOTS], (r * (SLOTS // EDGE_SLOTS) + k // EDGE_SLOTS + 1) * 16)
                parity = 0 if general else k % 2
                if pulled:
                    pe.wait_ge(pull_onehots, r * SLOTS + k + 1)
                    pulled_rows = pulled_ps[parity].rearrange("e i f -> e (i f)")
                    nc.tensor.matmul(pulled_rows, edges[:, k % EDGE_SLOTS, PULLED * TILE:], w_edge_wide[:],
                                     start=True, stop=False)
                    for b in range(BLOCKS):
                        nc.tensor.matmul(pulled_rows, pull_onehot[:, k % 2, b, :],
                                         h1_parts[:, b].rearrange("s i f -> s (i f)"),
                                         start=False, stop=(b == BLOCKS - 1))
                for half, tiles in enumerate(MESSAGE_TILES):
                    for j in tiles if not pulled or half == 0 else tiles[:-1]:
                        last = nc.tensor.matmul(edge_ps[parity][half][:, j - tiles.start],
                                                edges[:, k % EDGE_SLOTS, j * TILE:(j + 1) * TILE],
                                                w_edge_sb, start=True, stop=True)
                last.then_inc(edge_terms, 1)

            def scatter_group(layer, r, k, general, first=False):
                group = r * SLOTS + k
                if layer == 0:
                    lhs, lhs_there = (lambda j: rows[:, k, j, :]), (gathered[0][k], (r + 1) * 16 * TILES_PER_GROUP)
                    later = {}
                else:
                    if general:
                        edge_products(r, k, pulled=False, general=True)
                    lhs, lhs_there = (lambda j: message[:, j, :]), (message_ready, 2 * group + 1)
                    later = {MESSAGE_TILES[1].start: (message_ready, 2 * group + 2)}
                width = ROW if layer == 0 else FEAT
                if not general:
                    pe.wait_ge(*lhs_there)
                    pe.wait_ge(onehot_ready[layer], (r * DENSE_K + k if layer == 0 else group) + 1)
                    if layer == 0 and not first:
                        pe.wait_ge(window_added, r * SLOTS + k)
                    scatter(width, lhs, place(layer, k), scattered[layer], later)
                else:
                    with pe.Fori(0, N_WINDOWS) as w:
                        pe.wait_ge(*lhs_there)
                        pe.wait_ge(pass_onehot, (layer * N_GROUPS + group) * N_WINDOWS + w + 1)
                        scatter(width, lhs, 0, pass_scattered, later)

            def finish_chunk(c):
                pe.wait_ge(sums_done, [r1 for _, r1, _ in SPANS].index(CHUNK_COMPLETE[c]) + 1)
                if c > 0:
                    pe.wait_ge(node_sums_read, c)
                for j, b in enumerate(CHUNKS[c]):
                    last = nc.tensor.matmul(node_ps(SUMS_BANK, c, ROW)[:, j, :],
                                            sums[0][:, b * PARTS:(b + 1) * PARTS],
                                            w_neigh_sb[:], start=True, stop=True)
                last.then_inc(neigh_done, 1)

            def mlp_stage(c, stage):
                if stage == 0:
                    pe.wait_ge(hT_summed, c + 1)
                    if c > 0:
                        pe.wait_ge(h2_ready, 2 * c)
                    for half in range(2):
                        nc.tensor.matmul(half_ps(mm1_banks[half], c, half), w1_sb[:], hT[:, half_columns(c, half)],
                                         start=True, stop=True).then_inc(mm1_done, 1)
                else:
                    for half in range(2):
                        pe.wait_ge(r1_ready, 2 * c + half + 1)
                        nc.tensor.matmul(half_ps(mm2_banks[half], c, half), w2_sb[:], r1T[:, half_columns(c, half)],
                                         start=True, stop=True).then_inc(mm2_done, 1)

            def message_group(r, k, last_round=False):
                if k < SLOTS - 1 or not last_round:
                    ahead = next_group(r, k, 1)
                    edge_products(*ahead, is_pulled(ahead[1], last_round), general=False)
                scatter_group(1, r, k, general=False)

            def count_edges(r, first_round):
                pe.wait_ge(dst_onehot_ready, r + 1)
                for j in range(TILES_PER_GROUP):
                    pe.wait_ge(src_onehot_ready, r * TILES_PER_GROUP + j + 1)
                    for first in range(0, N_NODES, BANK):
                        if j == 0 and first + BANK >= N_NODES and not first_round:
                            pe.wait_ge(dense_reduced, r)
                        here = slice(first, min(first + BANK, N_NODES))
                        last = nc.tensor.matmul(counts_ps[:, here], dst_onehot[:, j, :],
                                                src_onehot[:, j % SRC_BUFFERS, here],
                                                start=(j == 0), stop=(j == TILES_PER_GROUP - 1))
                    last.then_inc(src_onehot_free, 1)
                nc.tensor.drain().then_inc(counted, 1)

            def transpose_counts(r):
                pe.wait_ge(identity_copied, 1)
                pe.wait_ge(counts_copied, r + 1)
                for n, (b0, b1_) in enumerate(countsT_chunks):
                    for b in range(b0, b1_):
                        last = nc.tensor.transpose(countsT_ps(n)[:, b - b0, :],
                                                   counts[:, b * PARTS:(b + 1) * PARTS], identity_h[:])
                last.then_inc(countsT_done, 1)

            def multiply_counts(r):
                pe.wait_ge(part_made, 3)
                pe.wait_ge(countsT_copied, r + 1)
                for b in range(BLOCKS):
                    last = nc.tensor.matmul(dense_ps, countsT[:, b, :], h_parts[:, b].rearrange("s i f -> s (i f)"),
                                            start=(b == 0), stop=(b == BLOCKS - 1))
                last.then_inc(dense_done, 1)

            def late_windows(r):
                pe.wait_ge(dense_reduced, r + 1)
                pe.wait_ge(window_added, r * SLOTS + 2)
                nc.tensor.transpose(window_ps[DENSE_K][0:ROW], dense_sum[:], identity[0:WINDOW, 0:WINDOW])
                scatter_group(0, r, DENSE_K - 1, general=False)

            def dense_round(r, span=None):
                own, complete_chunks = ((), ()) if span is None else (SELF_TERMS[span], SPANS[span][2])
                first = span == 0
                count_edges(r, first)
                if not first:
                    late_windows(r - 1)
                scatter_group(0, r, 0, general=False, first=first)
                transpose_counts(r)
                for c in own[:1]:
                    transpose_for_self(c)
                for c in complete_chunks[:1]:
                    finish_chunk(c)
                scatter_group(0, r, 1, general=False)
                for c in own[:1]:
                    self_term(c)
                for c in complete_chunks[1:]:
                    finish_chunk(c)
                for c in own[1:]:
                    transpose_for_self(c)
                multiply_counts(r)
                for c in own[1:]:
                    self_term(c)

            pe.wait_ge(routing_ready, 1)
            odd = pe.value_load(odd_i[0:1, 0:1], min_val=0, max_val=2 * N_GROUPS)
            for layer in range(2):
                if layer == 1:
                    for c in range(N_CHUNKS):
                        transpose_h(1, c)
                    pe.wait_ge(hT_copied, 4 * N_CHUNKS)
                with pe.If(odd):
                    if layer == 0:
                        for c in range(N_CHUNKS):
                            transpose_for_self(c)
                            self_term(c)
                    with pe.Fori(0, ROUNDS) as r:
                        for k in range(SLOTS):
                            scatter_group(layer, r, k, general=True)
                    for c in range(N_CHUNKS):
                        if layer == 0:
                            finish_chunk(c)
                        else:
                            for stage in range(2):
                                mlp_stage(c, stage)
                with pe.Else():
                    if layer == 1:
                        pe.wait_ge(h1_part[2], N_CHUNKS)
                        edge_products(0, 0, pulled=True, general=False)
                    for span, (r0, r1, chunks) in enumerate(SPANS):
                        if layer == 0:
                            dense_round(r0, span)
                            if r0 + 1 < r1:
                                with pe.Fori(r0 + 1, r1) as r:
                                    dense_round(r)
                        else:
                            for k in range(SLOTS):
                                message_group(r0, k, r0 == ROUNDS - 1)
                                for c, stage in mlp_stages(chunks, k):
                                    mlp_stage(c, stage)
                            if r0 + 1 < r1:
                                with pe.Fori(r0 + 1, r1) as r:
                                    for k in range(SLOTS):
                                        message_group(r, k)
                    if layer == 0:
                        late_windows(ROUNDS - 1)
                        finish_chunk(N_CHUNKS - 1)
                    else:
                        for stage in range(2):
                            mlp_stage(N_CHUNKS - 1, stage)

            for c in range(N_CHUNKS):
                pe.wait_ge(resultT_ready, c + 1)
                for j, b in enumerate(CHUNKS[c]):
                    last = nc.tensor.transpose(node_ps(RESULT_BANK + c, c, FEAT)[:, j, :],
                                               r1T[:, b * PARTS:(b + 1) * PARTS],
                                               identity[0:FEAT, 0:FEAT])
                last.then_inc(result_done, 1)


def kernel(x, src, dst, edge_attr_32, L0_gnn_W, L0_gnn_B, L1_gnn_We, L1_gnn_be, L1_gnn_W1, L1_gnn_b1,
           L1_gnn_W2, L1_gnn_b2, L1_gnn_gamma, L1_gnn_beta):
    import numpy as np
    import concourse.bacc as bacc
    from concourse.bass_utils import run_bass_kernel_spmd

    pad = PADDED_EDGES - N_EDGES
    src_p = np.pad(np.asarray(src), (0, pad))
    dst_p = np.pad(np.asarray(dst), (0, pad), mode="edge")
    edge_p = np.pad(np.asarray(edge_attr_32), ((0, pad), (0, 0)))
    arrays = {
        "x": np.asarray(x),
        "src": src_p.reshape(N_TILES, TILE).T,
        "dst": dst_p.reshape(N_TILES, TILE).T,
        "dst_grouped": dst_p.reshape(N_GROUPS, GROUP),
        "edge_attr": edge_p.reshape(N_GROUPS, GROUP, EDGE_FEAT).transpose(0, 2, 1),
        "w_neigh": np.asarray(L0_gnn_W).T,
        "w_self": np.asarray(L0_gnn_B).T,
        "w_edge": np.asarray(L1_gnn_We),
        "b_edge": np.asarray(L1_gnn_be).reshape(1, FEAT),
        "w1": np.asarray(L1_gnn_W1),
        "b1": np.asarray(L1_gnn_b1).reshape(FEAT, 1),
        "w2": np.asarray(L1_gnn_W2),
        "b2": np.asarray(L1_gnn_b2).reshape(FEAT, 1),
        "gamma": np.asarray(L1_gnn_gamma).reshape(FEAT, 1),
        "beta": np.asarray(L1_gnn_beta).reshape(FEAT, 1),
    }
    groups = np.arange(TILE)
    complete_before = sum(len(CHUNKS[c]) * PARTS * (groups >= CHUNK_COMPLETE[c] * SLOTS)
                          for c in range(N_CHUNKS - 1))
    nodes = np.arange(BLOCKS) * PARTS + groups[:, None]
    arrays["constants"] = np.concatenate([
        np.eye(TILE), np.tile(np.arange(WINDOW), (TILE, 1)), np.tile(np.arange(N_WINDOWS) * WINDOW, (TILE, 1)),
        complete_before[:, None], nodes], axis=1).astype(np.float32)
    arrays["source_numbers"] = (np.arange(SRC_PITCH) - SRC_SHIFT).astype(np.float16).reshape(1, SRC_PITCH)
    arrays["pulled_sources"] = src_p.reshape(N_GROUPS, GROUP)[:, -TILE:]
    arrays = {name: np.ascontiguousarray(a) for name, a in arrays.items()}
    nc = bacc.Bacc("TRN2", target_bir_lowering=False, num_devices=1)
    args = [nc.dram_tensor(name, a.shape, mybir.dt.from_np(a.dtype), kind="ExternalInput").ap()
            for name, a in arrays.items()]
    out = nc.dram_tensor("out", (N_NODES, FEAT), mybir.dt.float32, kind="ExternalOutput").ap()
    gnn_two_layers(nc, *args, out)
    result = run_bass_kernel_spmd(nc, [arrays], core_ids=[0])
    return result.results[0]["out"]
```
